# Optimizing a Trainium2 kernel written in Bass

```python
import numpy as np
import jax
import jax.numpy as jnp

def _softmax(x, axis=-1):
    return jax.nn.softmax(x, axis=axis)
def _gelu(x):
    return jax.nn.gelu(x, approximate=True)
def _silu(x):
    return jax.nn.silu(x)
def _sigmoid(x):
    return jax.nn.sigmoid(x)
def _layernorm(x, axis=-1, eps=1e-5):
    m = jnp.mean(x, axis=axis, keepdims=True)
    v = jnp.var(x, axis=axis, keepdims=True)
    return (x - m) / jnp.sqrt(v + eps)
def _scatter_add(tgt, idx, src, axis=0):
    return tgt.at[idx].add(src)
def _segment_sum(src, seg, n):
    return jax.ops.segment_sum(src, seg, n)

kernel_name = 'mk_adj_ffn_d1_adj_256_cb96c7'

def setup_inputs(seed: int = 0):
    np.random.seed(seed)
    _w = jnp.asarray
    def _rec_inputs():
        import jax
        import jax.numpy as jnp
        _gk = jax.random.key(seed)
        x = -0.0003929 + 0.9999 * jax.random.normal(jax.random.fold_in(_gk, 1), (32, 512, 256), jnp.float32)
        _a = jax.random.bernoulli(jax.random.fold_in(_gk, 2), 0.0625, (32, 512, 512))
        _a = jnp.logical_or(_a, jnp.swapaxes(_a, -1, -2))
        _a = jnp.logical_or(_a, jnp.eye(512, dtype=bool))
        _af = _a.astype(jnp.float32)
        adj = _af
        return x, adj
    x, adj = _rec_inputs()
    def _L0_gnn_setup():
        import jax, jax.numpy as jnp
        import numpy as np
        NEG = 9000000000000000.0
        key = jax.random.key(seed)
        ks = jax.random.split(key, 7)
        B, N, DIN, H, DOUT = (128, 512, 256, 256, 256)
        x = jax.random.normal(ks[0], (B, N, DIN), dtype=jnp.float32)
        mask = (jax.random.uniform(ks[1], (B, N, N)) > 0.5).astype(jnp.float32)

        def lin(k, fan_in, fan_out):
            kw, kb = jax.random.split(k)
            bound = 1.0 / np.sqrt(fan_in)
            W = jax.random.uniform(kw, (fan_in, fan_out), minval=-bound, maxval=bound, dtype=jnp.float32)
            b = jax.random.uniform(kb, (fan_out,), minval=-bound, maxval=bound, dtype=jnp.float32)
            return (W, b)
        Wv, bv = lin(ks[2], DIN, H)
        Wk, bk = lin(ks[3], DIN, H)
        Wq, bq = lin(ks[4], DIN, H)
        Wo, bo = lin(ks[5], H, DOUT)
        return {'x': x, 'mask': mask, 'Wv': Wv, 'bv': bv, 'Wk': Wk, 'bk': bk, 'Wq': Wq, 'bq': bq, 'Wo': Wo, 'bo': bo}
    _L0_gnn_all = _L0_gnn_setup()
    _L0_gnn_in = {k: v for k, v in _L0_gnn_all.items() if k in ('Wv', 'bv', 'Wk', 'bk', 'Wq', 'bq', 'Wo', 'bo', )}
    del _L0_gnn_all

    def _L0_ffn_setup():
        import jax, jax.numpy as jnp
        import numpy as np
        NUM_EXPERTS = 8
        TOP_K = 2
        B, S, D = (8, 8192, 256)

        def _moe(tokens, router_w, w1, b1, w2, b2):
            N = tokens.shape[0]
            E = router_w.shape[0]
            logits = tokens.astype(jnp.float32) @ router_w.astype(jnp.float32).T
            probs = jax.nn.softmax(logits, axis=-1)
            rw, re = jax.lax.top_k(probs, TOP_K)
            if TOP_K > 1:
                rw = rw / jnp.maximum(rw.sum(-1, keepdims=True), 1e-12)
            rw = rw.astype(tokens.dtype)
            combine = jnp.zeros((N, E), tokens.dtype).at[jnp.arange(N)[:, None], re].set(rw)
            out = tokens
            for e in range(E):
                h = jax.nn.gelu(tokens @ w1[e] + b1[e], approximate=False)
                y = h @ w2[e] + b2[e]
                out = out + combine[:, e:e + 1] * y
            return out
        key = jax.random.key(seed)
        ks = jax.random.split(key, 4)
        scale = 1.0 / np.sqrt(D).astype(np.float32)
        return {'input_embeddings': jax.random.normal(ks[0], (B, S, D), jnp.float32), 'router_w': jax.random.normal(ks[1], (NUM_EXPERTS, D), jnp.float32) * scale, 'w1': jax.random.normal(ks[2], (NUM_EXPERTS, D, D), jnp.float32) * scale, 'b1': jnp.zeros((NUM_EXPERTS, D), jnp.float32), 'w2': jax.random.normal(ks[3], (NUM_EXPERTS, D, D), jnp.float32) * scale, 'b2': jnp.zeros((NUM_EXPERTS, D), jnp.float32)}
    _L0_ffn_all = _L0_ffn_setup()
    _L0_ffn_in = {k: v for k, v in _L0_ffn_all.items() if k in ('router_w', 'w1', 'b1', 'w2', 'b2', )}
    del _L0_ffn_all

    return {
        "x": x,
        "adj": adj,
        "L0_gnn_Wv": _L0_gnn_in["Wv"],
        "L0_gnn_bv": _L0_gnn_in["bv"],
        "L0_gnn_Wk": _L0_gnn_in["Wk"],
        "L0_gnn_bk": _L0_gnn_in["bk"],
        "L0_gnn_Wq": _L0_gnn_in["Wq"],
        "L0_gnn_bq": _L0_gnn_in["bq"],
        "L0_gnn_Wo": _L0_gnn_in["Wo"],
        "L0_gnn_bo": _L0_gnn_in["bo"],
        "L0_ffn_router_w": _L0_ffn_in["router_w"],
        "L0_ffn_w1": _L0_ffn_in["w1"],
        "L0_ffn_b1": _L0_ffn_in["b1"],
        "L0_ffn_w2": _L0_ffn_in["w2"],
        "L0_ffn_b2": _L0_ffn_in["b2"],
    }

def reference(x, adj, L0_gnn_Wv, L0_gnn_bv, L0_gnn_Wk, L0_gnn_bk, L0_gnn_Wq, L0_gnn_bq, L0_gnn_Wo, L0_gnn_bo, L0_ffn_router_w, L0_ffn_w1, L0_ffn_b1, L0_ffn_w2, L0_ffn_b2):
    import jax
    import jax.numpy as jnp
    def _L0_gnn_ref(x, mask, Wv, bv, Wk, bk, Wq, bq, Wo, bo):
        import jax, jax.numpy as jnp
        import numpy as np
        NEG = 9000000000000000.0
        v = jax.nn.relu(jnp.einsum('bnd,dh->bnh', x, Wv) + bv)
        q = jax.nn.relu(jnp.einsum('bnd,dh->bnh', x, Wq) + bq)
        k = jax.nn.relu(jnp.einsum('bnd,dh->bnh', x, Wk) + bk)
        scores = jnp.einsum('bnh,bmh->bnm', q, k)
        att = jax.nn.softmax(scores * mask - NEG * (1.0 - mask), axis=2)
        out = jnp.einsum('bnm,bmh->bnh', att, v)
        out = jax.nn.relu(jnp.einsum('bnh,ho->bno', out, Wo) + bo)
        return out

    def _L0_ffn_ref(input_embeddings, router_w, w1, b1, w2, b2):
        import jax, jax.numpy as jnp
        import numpy as np
        NUM_EXPERTS = 8
        TOP_K = 2
        B, S, D = (8, 8192, 256)

        def _moe(tokens, router_w, w1, b1, w2, b2):
            N = tokens.shape[0]
            E = router_w.shape[0]
            logits = tokens.astype(jnp.float32) @ router_w.astype(jnp.float32).T
            probs = jax.nn.softmax(logits, axis=-1)
            rw, re = jax.lax.top_k(probs, TOP_K)
            if TOP_K > 1:
                rw = rw / jnp.maximum(rw.sum(-1, keepdims=True), 1e-12)
            rw = rw.astype(tokens.dtype)
            combine = jnp.zeros((N, E), tokens.dtype).at[jnp.arange(N)[:, None], re].set(rw)
            out = tokens
            for e in range(E):
                h = jax.nn.gelu(tokens @ w1[e] + b1[e], approximate=False)
                y = h @ w2[e] + b2[e]
                out = out + combine[:, e:e + 1] * y
            return out
        b, s, d = input_embeddings.shape
        tokens = input_embeddings.reshape(b * s, d)
        return _moe(tokens, router_w, w1, b1, w2, b2).reshape(b, s, d)

    x = x + _L0_gnn_ref(_layernorm(x, axis=-1), adj, L0_gnn_Wv, L0_gnn_bv, L0_gnn_Wk, L0_gnn_bk, L0_gnn_Wq, L0_gnn_bq, L0_gnn_Wo, L0_gnn_bo)
    x = x + _L0_ffn_ref(_layernorm(x, axis=-1), L0_ffn_router_w, L0_ffn_w1, L0_ffn_b1, L0_ffn_w2, L0_ffn_b2)
    return x


_drawn_inputs = setup_inputs


def setup_inputs(seed=0):
    import zlib

    import numpy as np

    out = dict(_drawn_inputs(seed))
    spreads = {'L0_ffn_b1': (0.0, 0.327), 'L0_ffn_b2': (0.0, 0.1)}
    factors = {'L0_gnn_bv': 3.247, 'L0_gnn_bk': 5.489, 'L0_gnn_bq': 4.226}
    for name, (base, spread) in spreads.items():
        noise = np.random.default_rng([zlib.crc32(name.encode()), seed]).standard_normal(out[name].shape)
        drawn = base * np.exp(spread * noise) if base else spread * noise
        out[name] = jnp.asarray(drawn.astype(out[name].dtype))
    for name, factor in factors.items():
        out[name] = (out[name] * factor).astype(out[name].dtype)
    return out
```

```python
from contextlib import ExitStack

import concourse.bass as bass
from concourse import mybir

P = 128
F32 = mybir.dt.float32
F32R = mybir.dt.float32r
BF16 = mybir.dt.bfloat16
U32 = mybir.dt.uint32
I32 = mybir.dt.int32
ALU = mybir.AluOpType
ACT = mybir.ActivationFunctionType
AX = mybir.AxisListType

NEG = 9000000000000000.0
EPS = 1e-5
BIG = 3.0e38


def build_program(nc, x, adj, wv, bv, wk, bk, wq, bq, wo, bo, router_w, w1, b1, w2, b2, out):
    G, N, D = x.shape
    E = router_w.shape[0]
    T = N // P
    C = D // P
    TOKENS = G * N
    BLOCK = 512
    REGION = TOKENS + BLOCK
    DUMMY = E * REGION
    NBLOCKS = (2 * TOKENS + E * (BLOCK - 1)) // BLOCK
    ID = D
    GATE = D + 1
    ROW = 272
    assert GATE + E <= ROW and N == BLOCK == 4 * P and D == 2 * P

    rows_dram = nc.dram_tensor("rows_dram", [DUMMY + BLOCK, ROW], F32, kind="Internal").ap()

    x_v = x.rearrange("g (p t) d -> (g p) (t d)", t=T)
    adj_v = adj.rearrange("g (p t) m -> (g p) (t m)", t=T)
    out_v = out.rearrange("(q t) d -> q (t d)", t=T)

    with ExitStack() as whole:
        def sb(stack, name, shape, dt):
            return stack.enter_context(nc.sbuf_tensor(name, shape, dt))

        def sem(name):
            return whole.enter_context(nc.semaphore(name))

        bank = [whole.enter_context(nc.psum_tensor(f"bank{i}", [P, 512], F32)) for i in range(8)]

        ident = sb(whole, "ident", [P, P], F32)
        ones = sb(whole, "ones", [P, 512], F32R)
        before = sb(whole, "before", [P, P], BF16)
        ones_bf = sb(whole, "ones_bf", [P, P], BF16)
        expert_no = sb(whole, "expert_no", [P, E], F32)
        carry = sb(whole, "carry", [P, E], F32)

        loaded = sem("loaded")
        waited_apart = sem("waited_apart")
        consts_made = sem("consts_made")

        def wait_apart(eng, what, value):
            eng.wait_ge(what, value)
            eng.sem_inc(waited_apart, 1)

        with ExitStack() as ph:
            w_hi = {n: sb(ph, f"w{n}_hi", [P, C, D], F32R) for n in "qkvo"}
            w_lo = {n: sb(ph, f"w{n}_lo", [P, C, D], F32R) for n in "qkvo"}
            bias = {n: sb(ph, f"bias_{n}", [P, D], F32R) for n in "qkv"}
            bo_rows = sb(ph, "bo_rows", [P, D], F32)
            router_rows = sb(ph, "router_rows", [E, D], F32)
            router_t = sb(ph, "router_t", [P, C, E], F32)
            minus_half = sb(ph, "minus_half", [P, T], F32)
            id_f = sb(ph, "id_f", [P, T], F32)

            x_norm = sb(ph, "x_norm", [P, T, D], F32)
            x_res = sb(ph, "x_res", [P, T, D], F32)
            adj_t = sb(ph, "adj_t", [P, T, N], F32)
            neg_mask = sb(ph, "neg_mask", [P, T, N], F32)
            xn = sb(ph, "xn", [P, T, D], F32)
            xnT_hi = sb(ph, "xnT_hi", [P, C, N], F32R)
            xnT_lo = sb(ph, "xnT_lo", [P, C, N], F32R)
            qk_hi = sb(ph, "qk_hi", [P, 2 * C, N], F32R)
            qk_lo = sb(ph, "qk_lo", [P, 2 * C, N], F32R)
            v_hi = sb(ph, "v_hi", [P, T, D], F32R)
            v_lo = sb(ph, "v_lo", [P, T, D], F32R)
            prob = sb(ph, "prob", [P, T, N], F32)
            probT_hi = sb(ph, "probT_hi", [P, T, N], F32R)
            probT_lo = sb(ph, "probT_lo", [P, T, N], F32R)
            oT_hi = sb(ph, "oT_hi", [P, C, N], F32R)
            oT_lo = sb(ph, "oT_lo", [P, C, N], F32R)
            y_sb = sb(ph, "y_sb", [P, T, D], F32)
            x1 = sb(ph, "x1", [P, T, D], F32)
            rows = sb(ph, "rows", [P, T, ROW], F32)
            xn2T = sb(ph, "xn2T", [P, C, N], F32)

            neg_max = sb(ph, "neg_max", [P, T], F32)
            row_sum = sb(ph, "row_sum", [P, T], F32)
            row_inv = sb(ph, "row_inv", [P, T], F32)
            st = {n: sb(ph, f"st{n}", [P, T, 6], F32) for n in "12"}
            mv = {n: sb(ph, f"mv{n}", [P, T, 2], F32) for n in "12"}
            var_eps = {n: sb(ph, f"var_eps{n}", [P, T], F32) for n in "12"}
            rstd = {n: sb(ph, f"rstd{n}", [P, T], F32) for n in "12"}

            logits = sb(ph, "logits", [P, T, E], F32)
            top8 = sb(ph, "top8", [P, T, 8], F32)
            top8_at = sb(ph, "top8_at", [P, T, 8], U32)
            top2_at = sb(ph, "top2_at", [P, T, 2], F32)
            is_top = sb(ph, "is_top", [P, 2, T, E], F32)
            chosen = sb(ph, "chosen", [P, T, E], F32)
            chosen_bf = sb(ph, "chosen_bf", [P, T, E], BF16)
            shifted = sb(ph, "shifted", [P, T, E], F32)
            expo = sb(ph, "expo", [P, T, E], F32)
            gate_sum = sb(ph, "gate_sum", [P, 4, T], F32)
            gates = sb(ph, "gates", [P, 2, T, E], F32)
            place = sb(ph, "place", [P, T, E], F32)
            place_top = sb(ph, "place_top", [P, 2, T, E], F32)
            slot_f = sb(ph, "slot_f", [P, 2, T], F32)
            slot = sb(ph, "slot", [P, 2, T], U32)

            xnorm_loaded = sem("xnorm_loaded")
            xres_loaded = sem("xres_loaded")
            adj_loaded = sem("adj_loaded")
            var1_ready = sem("var1_ready")
            rstd1_ready = sem("rstd1_ready")
            xn_ready = sem("xn_ready")
            xnT_psum = sem("xnT_psum")
            xnT_hi_ready = sem("xnT_hi_ready")
            xnT_lo_ready = sem("xnT_lo_ready")
            qk_psum = sem("qk_psum")
            qk_hi_ready = sem("qk_hi_ready")
            qk_lo_ready = sem("qk_lo_ready")
            v_psum = sem("v_psum")
            v_hi_ready = sem("v_hi_ready")
            v_lo_ready = sem("v_lo_ready")
            score_psum = sem("score_psum")
            negmask_ready = sem("negmask_ready")
            masked = sem("masked")
            shift_ready = sem("shift_ready")
            prob_ready = sem("prob_ready")
            probT_psum = sem("probT_psum")
            probT_hi_ready = sem("probT_hi_ready")
            probT_lo_ready = sem("probT_lo_ready")
            o_psum = sem("o_psum")
            o_hi_ready = sem("o_hi_ready")
            o_lo_ready = sem("o_lo_ready")
            inv_ready = sem("inv_ready")
            y_psum = sem("y_psum")
            y_ready = sem("y_ready")
            x1_ready = sem("x1_ready")
            var2_ready = sem("var2_ready")
            rstd2_ready = sem("rstd2_ready")
            xn2_ready = sem("xn2_ready")
            base_ready = sem("base_ready")
            base_stored = sem("base_stored")
            xn2T_psum = sem("xn2T_psum")
            xn2T_ready = sem("xn2T_ready")
            logits_psum = sem("logits_psum")
            logits_ready = sem("logits_ready")
            expo_in = sem("expo_in")
            expo_ready = sem("expo_ready")
            chosen_ready = sem("chosen_ready")
            rank_psum = sem("rank_psum")
            gates_ready = sem("gates_ready")
            slots_ready = sem("slots_ready")
            id_ready = sem("id_ready")
            id_step = sem("id_step")
            scattered = sem("scattered")
            stats_step = sem("stats_step")
            route_step = sem("route_step")
            ROUTE = 16
            hi_made = sem("hi_made")
            lo_made = sem("lo_made")
            bias_zeroed = sem("bias_zeroed")
            router_psum = sem("router_psum")
            router_made = sem("router_made")
            pool_step = sem("pool_step")
            pad_stored = sem("pad_stored")

            with nc.Block() as block:
                w_stage = {"q": prob[:, 0, :], "k": prob[:, 1, :], "v": prob[:, 2, :], "o": prob[:, 3, :]}
                b_stage = {"q": y_sb[:, 0, :], "k": y_sb[:, 1, :], "v": y_sb[:, 2, :]}
                w_in = {"q": wq, "k": wk, "v": wv, "o": wo}
                b_in = {"q": bq, "k": bk, "v": bv}
                SETUP_LOADS = 4 + 6 + 2

                @block.sync
                def _(sp):
                    for n in "qkvo":
                        sp.dma_start(w_stage[n].rearrange("p (c n) -> p c n", c=C),
                                     w_in[n].rearrange("(c p) n -> p c n", p=P)).then_inc(loaded, 16)
                    sp.wait_ge(bias_zeroed, 1)
                    for n in "qkv":
                        for row in (0, 32):
                            sp.dma_start(b_stage[n][row:row + 1, :], b_in[n].rearrange("(o n) -> o n", o=1)).then_inc(loaded, 16)
                    sp.dma_start(bo_rows[:], bo.partition_broadcast(P)).then_inc(loaded, 16)
                    sp.dma_start(router_rows[:], router_w).then_inc(loaded, 16)
                    sp.dma_start(x_norm[:].rearrange("p t d -> p (t d)"), x_v[0:P, :]).then_inc(xnorm_loaded, 16)
                    sp.dma_start(x_res[:].rearrange("p t d -> p (t d)"), x_v[0:P, :]).then_inc(xres_loaded, 16)
                    sp.dma_start(adj_t[:].rearrange("p t m -> p (t m)"), adj_v[0:P, :]).then_inc(adj_loaded, 16)
                    sp.wait_ge(xn_ready, 1)
                    sp.dma_start(x_norm[:].rearrange("p t d -> p (t d)"), x_v[P:2 * P, :]).then_inc(xnorm_loaded, 16)

                    def graph(g, first=False, load_next=True, load_after=True):
                        if load_next:
                            wait_apart(sp, masked, 4 * g + 4)
                            wait_apart(sp, negmask_ready, g + 1)
                            sp.dma_start(adj_t[:].rearrange("p t m -> p (t m)"),
                                         adj_v[bass.ds(g * P + P, P), :]).then_inc(adj_loaded, 16)
                        if not first:
                            wait_apart(sp, base_ready, g)
                            sp.dma_start(out_v[bass.ds(g * P - P, P), :],
                                         x1[:].rearrange("p t d -> p (t d)")).then_inc(base_stored, 16)
                        if load_after:
                            wait_apart(sp, xn_ready, g + 2)
                            sp.dma_start(x_norm[:].rearrange("p t d -> p (t d)"),
                                         x_v[bass.ds(g * P + 2 * P, P), :]).then_inc(xnorm_loaded, 16)
                        if load_next:
                            wait_apart(sp, x1_ready, 2 * g + 2)
                            sp.dma_start(x_res[:].rearrange("p t d -> p (t d)"),
                                         x_v[bass.ds(g * P + P, P), :]).then_inc(xres_loaded, 16)

                    graph(0, first=True)
                    with sp.Fori(1, G - 2) as g:
                        graph(g)
                    graph(G - 2, load_after=False)
                    graph(G - 1, load_next=False, load_after=False)
                    sp.wait_ge(base_ready, G)
                    sp.dma_start(out_v[(G - 1) * P:G * P, :], x1[:].rearrange("p t d -> p (t d)")).then_inc(base_stored, 16)
                    sp.wait_ge(base_stored, 16 * G)

                @block.gpsimd
                def _(pool):
                    pool.memset(ident[:], 0.0).then_inc(pool_step, 1)
                    pool.memset(before[:], 1.0).then_inc(pool_step, 1)
                    pool.memset(ones_bf[:], 1.0)
                    pool.memset(minus_half[:], -0.5)
                    for n in "qkv":
                        z = pool.memset(b_stage[n], 0.0)
                    z.then_inc(bias_zeroed, 1)
                    pool.memset(rows[:], 0.0).then_inc(pool_step, 1)
                    pool.iota(expert_no[:], [[1, E]], 0, 0, allow_small_or_imprecise_dtypes=True)
                    pool.iota(id_f[:], [[1, T]], 0, T, allow_small_or_imprecise_dtypes=True).then_inc(pool_step, 1)
                    pool.iota(carry[:], [[1, E]], 0, 0, allow_small_or_imprecise_dtypes=True).then_inc(pool_step, 1)
                    pool.wait_ge(pool_step, 5)
                    pool.affine_select(out=ident[:], in_=ident[:], compare_op=ALU.not_equal, fill=1.0, base=0,
                                       pattern=[[-1, P]], channel_multiplier=1)
                    pool.affine_select(out=before[:], in_=before[:], compare_op=ALU.is_gt, fill=0.0, base=0,
                                       pattern=[[1, P]], channel_multiplier=-1)
                    pool.tensor_scalar(carry[:], carry[:], float(REGION), 0.0, ALU.mult, ALU.add).then_inc(consts_made, 1)

                    def neg_of_mask(g):
                        wait_apart(pool, adj_loaded, 16 * g + 16)
                        pool.tensor_scalar(neg_mask[:].rearrange("q s (t p) -> q s t p", t=T), adj_t[:].rearrange("q s (p t) -> q s t p", t=T),
                                           -NEG, NEG, ALU.mult, ALU.add).then_inc(negmask_ready, 1)

                    def root(n, ready, done, k):
                        pool.wait_ge(ready, k)
                        pool.tensor_tensor(rstd[n][:], var_eps[n][:], minus_half[:], ALU.pow).then_inc(done, 1)

                    def write_ids(g, first):
                        if not first:
                            wait_apart(pool, scattered, 16 * 2 * T * g)
                        pool.tensor_copy(rows[:, :, ID].bitcast(U32), id_f[:]).then_inc(id_ready, 1)
                        wait_apart(pool, id_ready, g + 1)
                        pool.tensor_scalar(id_f[:], id_f[:], 1.0, float(N), ALU.mult, ALU.add).then_inc(id_step, 1)

                    def base(g, first):
                        pool.wait_ge(x1_ready, 2 * g + 2)
                        pool.wait_ge(xn2_ready, g + 1)
                        pool.tensor_tensor(x1[:], x1[:], rows[:, :, 0:D], ALU.add).then_inc(base_ready, 1)

                    def scatter(g):
                        wait_apart(pool, id_ready, g + 1)
                        wait_apart(pool, gates_ready, g + 1)
                        wait_apart(pool, slots_ready, g + 1)
                        for t in range(T):
                            for k in range(2):
                                pool.indirect_dma_start(
                                    rows_dram, bass.IndirectOffsetOnAxis(ap=slot[:, k, t:t + 1], axis=0),
                                    rows[:, t, :], None).then_inc(scattered, 16)

                    root("1", var1_ready, rstd1_ready, 1)
                    neg_of_mask(0)

                    def graph(g, first=False, last=False, second=False):
                        if not first:
                            root("2", var2_ready, rstd2_ready, g)
                        if not last:
                            root("1", var1_ready, rstd1_ready, g + 2)
                        if not first:
                            write_ids(g - 1, second)
                            base(g - 1, second)
                        if not last:
                            wait_apart(pool, shift_ready, 4 * g + 4)
                            neg_of_mask(g + 1)
                        if not first:
                            scatter(g - 1)

                    graph(0, first=True)
                    graph(1, second=True)
                    with pool.Fori(2, G - 1) as g:
                        graph(g)
                    graph(G - 1, last=True)
                    root("2", var2_ready, rstd2_ready, G)
                    write_ids(G - 1, False)
                    base(G - 1, False)
                    scatter(G - 1)
                    pool.wait_ge(scattered, 16 * 2 * T * G)

                @block.scalar
                def _(act):
                    for n in "qkvo":
                        act.wait_ge(loaded, 16 * SETUP_LOADS)
                        act.copy(w_hi[n][:].rearrange("p c n -> p (c n)"), w_stage[n]).then_inc(hi_made, 1)
                    for n in "qkv":
                        act.copy(bias[n][:], b_stage[n]).then_inc(hi_made, 1)

                    def xnT(g):
                        for c in range(C):
                            act.wait_ge(xnT_psum, 2 * g + c + 1)
                            act.copy(xnT_hi[:, c, :], bank[2 + c][:]).then_inc(xnT_hi_ready, 1)

                    def qk(g):
                        for u in range(2 * C):
                            act.wait_ge(qk_psum, 4 * g + u + 1)
                            act.activation(qk_hi[:, u, :], bank[(2 + u) % 4][:], ACT.Relu).then_inc(qk_hi_ready, 1)

                    def route_copy(g):
                        for c in range(C):
                            act.wait_ge(xn2T_psum, 2 * g + c + 1)
                            act.copy(xn2T[:, c, :], bank[2 + c][:]).then_inc(xn2T_ready, 1)

                    def route_exp(g):
                        act.wait_ge(expo_in, g + 1)
                        act.activation(expo[:], shifted[:], ACT.Exp).then_inc(expo_ready, 1)

                    xnT(0)
                    qk(0)

                    def graph(g, first=False, last=False):
                        if not first:
                            act.wait_ge(inv_ready, g)
                        for t in range(T):
                            act.wait_ge(shift_ready, 4 * g + t + 1)
                            act.activation(prob[:, t, :], prob[:, t, :], ACT.Exp, bias=neg_max[:, t:t + 1], scale=-1.0,
                                           accum_out=row_sum[:, t:t + 1]).then_inc(prob_ready, 1)
                        for i in range(2):
                            act.wait_ge(v_psum, 2 * g + i + 1)
                            act.activation(v_hi[:, 2 * i:2 * i + 2, :].rearrange("p t d -> p (t d)"), bank[i][:],
                                           ACT.Relu).then_inc(v_hi_ready, 1)
                        if not first:
                            route_copy(g - 1)
                        if not last:
                            xnT(g + 1)
                        if not first:
                            route_exp(g - 1)
                        for m in range(T):
                            act.wait_ge(probT_psum, 4 * g + m + 1)
                            act.copy(probT_hi[:, m, :], bank[4 + m][:]).then_inc(probT_hi_ready, 1)
                        for c in range(C):
                            act.wait_ge(o_psum, 2 * g + c + 1)
                            act.copy(oT_hi[:, c, :], bank[c][:]).then_inc(o_hi_ready, 1)
                        if not last:
                            qk(g + 1)

                    graph(0, first=True)
                    with act.Fori(1, G - 1) as g:
                        graph(g)
                    graph(G - 1, last=True)
                    route_copy(G - 1)
                    route_exp(G - 1)

                @block.vector
                def _(dve):
                    dve.wait_ge(consts_made, 1)
                    dve.memset(ones[:].bitcast(F32), 1.0)
                    dve.wait_ge(loaded, 16 * SETUP_LOADS)
                    for i, n in enumerate("qkvo"):
                        dve.wait_ge(hi_made, i + 1)
                        dve.tensor_tensor(w_lo[n][:].rearrange("p c n -> p (c n)"), w_stage[n],
                                          w_hi[n][:].bitcast(F32).rearrange("p c n -> p (c n)"), ALU.subtract).then_inc(lo_made, 1)
                    dve.wait_ge(hi_made, 7)
                    for n in "qkv":
                        dve.tensor_tensor(bias[n][32:33, :], b_stage[n][32:33, :], bias[n][32:33, :].bitcast(F32),
                                          ALU.subtract).then_inc(lo_made, 1)
                    dve.wait_ge(router_psum, 1)
                    dve.tensor_copy(router_t[:].rearrange("p c e -> p (c e)"), bank[7][:, 0:C * E]).then_inc(router_made, 1)

                    def lo_of(dst, src, hi, relu):
                        if relu:
                            return dve.scalar_tensor_tensor(dst, src, 0.0, hi.bitcast(F32), ALU.max, ALU.subtract)
                        return dve.tensor_tensor(dst, src, hi.bitcast(F32), ALU.subtract)

                    def norm_stats(n, src, k, ready):
                        for t in range(T):
                            i = dve.bn_stats(st[n][:, t, :], src[:, t, :])
                        i.then_inc(stats_step, 1)
                        wait_apart(dve, stats_step, 2 * k + 1)
                        for t in range(T):
                            i = dve.bn_aggr(mv[n][:, t, :], st[n][:, t, :])
                        i.then_inc(stats_step, 1)
                        dve.wait_ge(stats_step, 2 * k + 2)
                        dve.tensor_scalar(var_eps[n][:], mv[n][:, :, 1], EPS, None, ALU.add).then_inc(ready, 1)

                    def norm_apply(n, dst, src):
                        for t in range(T):
                            i = dve.tensor_scalar(dst[:, t, 0:D], src[:, t, :], mv[n][:, t, 0:1], rstd[n][:, t:t + 1],
                                                  ALU.subtract, ALU.mult)
                        return i

                    def stats1(g, k):
                        dve.wait_ge(xnorm_loaded, 16 * g + 16)
                        norm_stats("1", x_norm, k, var1_ready)

                    def apply1(g, prev):
                        dve.wait_ge(rstd1_ready, g + 1)
                        if prev:
                            dve.wait_ge(xnT_psum, 2 * g)
                        norm_apply("1", xn, x_norm).then_inc(xn_ready, 1)

                    def stats2(g, k):
                        dve.wait_ge(x1_ready, 2 * g + 2)
                        norm_stats("2", x1, k, var2_ready)

                    def apply2(g, prev):
                        dve.wait_ge(rstd2_ready, g + 1)
                        if prev:
                            dve.wait_ge(scattered, 16 * 2 * T * g)
                        norm_apply("2", rows, x1).then_inc(xn2_ready, 1)

                    def xnT(g):
                        for c in range(C):
                            dve.wait_ge(xnT_hi_ready, 2 * g + c + 1)
                            lo_of(xnT_lo[:, c, :], bank[2 + c][:], xnT_hi[:, c, :], False).then_inc(xnT_lo_ready, 1)

                    def qk(g):
                        for u in range(2 * C):
                            dve.wait_ge(qk_hi_ready, 4 * g + u + 1)
                            lo_of(qk_lo[:, u, :], bank[(2 + u) % 4][:], qk_hi[:, u, :], True).then_inc(qk_lo_ready, 1)

                    def route_choose(g):
                        step = [0]

                        def then(i):
                            step[0] += 1
                            i.then_inc(route_step, 1)
                            dve.wait_ge(route_step, ROUTE * g + step[0])

                        def wide(ap):
                            return ap.to_broadcast([P, T, E])

                        dve.wait_ge(logits_psum, g + 1)
                        step[0] += 1
                        dve.tensor_copy(logits[:].rearrange("p t e -> p (t e)"), bank[0][:, 0:T * E]).then_inc(route_step, 1)
                        wait_apart(dve, route_step, ROUTE * g + step[0])
                        for t in range(T):
                            i = dve.max(top8[:, t, :], logits[:, t, :])
                        then(i)
                        dve.tensor_tensor(shifted[:], logits[:], wide(top8[:, :, 0:1]), ALU.subtract).then_inc(expo_in, 1)
                        dve.wait_ge(consts_made, 1)
                        for t in range(T):
                            i = dve.max_index(top8_at[:, t, :], top8[:, t, :], logits[:, t, :])
                        then(i)
                        then(dve.tensor_copy(top2_at[:], top8_at[:, :, 0:2]))
                        for k in range(2):
                            i = dve.tensor_tensor(is_top[:, k], expert_no[:].unsqueeze(1).to_broadcast([P, T, E]),
                                                  wide(top2_at[:, :, k:k + 1]), ALU.is_equal)
                        then(i)
                        dve.tensor_tensor(chosen_bf[:], is_top[:, 0], is_top[:, 1], ALU.add).then_inc(chosen_ready, 1)
                        then(dve.tensor_tensor(chosen[:], is_top[:, 0], is_top[:, 1], ALU.add))
                        dve.wait_ge(expo_ready, g + 1)
                        then(dve.tensor_reduce(gate_sum[:, 0, :], expo[:], AX.X, ALU.add))
                        then(dve.reciprocal(gate_sum[:, 1, :], gate_sum[:, 0, :]))
                        then(dve.tensor_tensor(gates[:, 0], expo[:], wide(gate_sum[:, 1, :].unsqueeze(2)), ALU.mult))
                        then(dve.tensor_tensor(gates[:, 1], gates[:, 0], chosen[:], ALU.mult))
                        then(dve.tensor_reduce(gate_sum[:, 2, :], gates[:, 1], AX.X, ALU.add))
                        then(dve.tensor_scalar(gate_sum[:, 3, :], gate_sum[:, 2, :], 1e-12, None, ALU.max))
                        then(dve.reciprocal(gate_sum[:, 2, :], gate_sum[:, 3, :]))
                        dve.tensor_tensor(rows[:, :, GATE:GATE + E], gates[:, 1], wide(gate_sum[:, 2, :].unsqueeze(2)),
                                          ALU.mult).then_inc(gates_ready, 1)
                        return step[0]

                    def route_place(g, done):
                        dve.wait_ge(rank_psum, g + 1)
                        ranks = bank[1][:, 0:T * E].rearrange("p (t e) -> p t e", t=T)
                        dve.tensor_tensor(place[:], ranks, carry[:].unsqueeze(1).to_broadcast([P, T, E]),
                                          ALU.add).then_inc(route_step, 1)
                        dve.wait_ge(route_step, ROUTE * g + done + 1)
                        dve.tensor_tensor(carry[:], carry[:], bank[1][:, T * E:(T + 1) * E], ALU.add)
                        for k in range(2):
                            i = dve.tensor_tensor(place_top[:, k], place[:], is_top[:, k], ALU.mult)
                        i.then_inc(route_step, 1)
                        dve.wait_ge(route_step, ROUTE * g + done + 2)
                        dve.tensor_reduce(slot_f[:], place_top[:], AX.X, ALU.add).then_inc(route_step, 1)
                        assert done + 3 == ROUTE
                        dve.wait_ge(route_step, ROUTE * g + ROUTE)
                        dve.tensor_copy(slot[:], slot_f[:]).then_inc(slots_ready, 1)

                    stats1(0, 0)
                    apply1(0, False)
                    xnT(0)
                    qk(0)

                    def graph(g, first=False, last=False):
                        k = 1 if first else 2 * g
                        if not first:
                            stats2(g - 1, k)
                            k = k + 1
                        if not first:
                            dve.wait_ge(probT_psum, 4 * g)
                        dve.wait_ge(adj_loaded, 16 * g + 16)

                        def times_mask(t):
                            dve.wait_ge(score_psum, 4 * g + t + 1)
                            dve.scalar_tensor_tensor(
                                prob[:, t, :].rearrange("q (t p) -> q t p", t=T),
                                bank[4 + t][:].rearrange("q (t p) -> q t p", t=T), -1.0,
                                adj_t[:, t, :].rearrange("q (p t) -> q t p", t=T), ALU.mult, ALU.mult).then_inc(masked, 1)

                        def add_mask(t):
                            wait_apart(dve, masked, 4 * g + t + 1)
                            dve.tensor_tensor_reduce(prob[:, t, :], prob[:, t, :], neg_mask[:, t, :], 1.0, BIG, ALU.add,
                                                     ALU.min, neg_max[:, t:t + 1]).then_inc(shift_ready, 1)

                        times_mask(0)
                        dve.wait_ge(negmask_ready, g + 1)
                        for t in range(1, T):
                            times_mask(t)
                            add_mask(t - 1)
                        add_mask(T - 1)
                        if not first:
                            apply2(g - 1, True)
                        if not last:
                            stats1(g + 1, k)
                        for i in range(2):
                            dve.wait_ge(v_hi_ready, 2 * g + i + 1)
                            lo_of(v_lo[:, 2 * i:2 * i + 2, :].rearrange("p t d -> p (t d)"), bank[i][:],
                                  v_hi[:, 2 * i:2 * i + 2, :].rearrange("p t d -> p (t d)"), True).then_inc(v_lo_ready, 1)
                        if not last:
                            apply1(g + 1, True)
                        if not first:
                            done = route_choose(g - 1)
                        if not last:
                            xnT(g + 1)
                        if not first:
                            route_place(g - 1, done)
                        dve.wait_ge(prob_ready, 4 * g + 4)
                        dve.reciprocal(row_inv[:], row_sum[:]).then_inc(inv_ready, 1)
                        for m in range(T):
                            dve.wait_ge(probT_hi_ready, 4 * g + m + 1)
                            lo_of(probT_lo[:, m, :], bank[4 + m][:], probT_hi[:, m, :], False).then_inc(probT_lo_ready, 1)
                        for c in range(C):
                            dve.wait_ge(o_hi_ready, 2 * g + c + 1)
                            lo_of(oT_lo[:, c, :], bank[c][:], oT_hi[:, c, :], False).then_inc(o_lo_ready, 1)
                        if not last:
                            qk(g + 1)
                        dve.wait_ge(inv_ready, g + 1)
                        if not first:
                            dve.wait_ge(base_stored, 16 * g)
                        dve.wait_ge(xres_loaded, 16 * g + 16)
                        for i in range(2):
                            dve.wait_ge(y_psum, 2 * g + i + 1)
                            for j in range(2):
                                t = 2 * i + j
                                dve.scalar_tensor_tensor(y_sb[:, t, :], bank[2 + i][:, j * D:(j + 1) * D], row_inv[:, t:t + 1],
                                                         bo_rows[:], ALU.mult, ALU.add).then_inc(y_ready, 1)
                        for i in range(2):
                            dve.wait_ge(y_ready, 4 * g + 2 * i + 2)
                            dve.scalar_tensor_tensor(x1[:, 2 * i:2 * i + 2, :], y_sb[:, 2 * i:2 * i + 2, :], 0.0,
                                                     x_res[:, 2 * i:2 * i + 2, :], ALU.max, ALU.add).then_inc(x1_ready, 1)

                    graph(0, first=True)
                    with dve.Fori(1, G - 1) as g:
                        graph(g)
                    graph(G - 1, last=True)
                    stats2(G - 1, 2 * G - 1)
                    apply2(G - 1, True)
                    done = route_choose(G - 1)
                    route_place(G - 1, done)

                @block.tensor
                def _(pe):
                    pe.wait_ge(consts_made, 1)
                    pe.wait_ge(loaded, 16 * SETUP_LOADS)
                    for c in range(C):
                        i = pe.transpose(bank[7][:, c * E:(c + 1) * E], router_rows[:, c * P:(c + 1) * P], ident[0:E, 0:E])
                    i.then_inc(router_psum, 1)
                    pe.wait_ge(lo_made, 7)
                    pe.wait_ge(router_made, 1)

                    def split3(dst, a_hi, a_lo, b_hi, b_lo, start, stop):
                        pe.matmul(dst, a_hi, b_hi, start=start, stop=False)
                        pe.matmul(dst, a_hi, b_lo, start=False, stop=False)
                        return pe.matmul(dst, a_lo, b_hi, start=False, stop=stop)

                    def xnT(g):
                        pe.wait_ge(xn_ready, g + 1)
                        for c in range(C):
                            for t in range(T):
                                i = pe.transpose(bank[2 + c][:, t * P:(t + 1) * P], xn[:, t, c * P:(c + 1) * P], ident[:])
                            i.then_inc(xnT_psum, 1)

                    def qk(g):
                        pe.wait_ge(xnT_hi_ready, 2 * g + 2)
                        pe.wait_ge(xnT_lo_ready, 2 * g + 2)
                        for u in range(2 * C):
                            n, h = "qk"[u // C], u % C
                            if u == C:
                                pe.wait_ge(o_lo_ready, 2 * g)
                            dst = bank[(2 + u) % 4][:]
                            pe.matmul(dst, bias[n][:, h * P:(h + 1) * P], ones[:], start=True, stop=False)
                            for c in range(C):
                                i = split3(dst, w_hi[n][:, c, h * P:(h + 1) * P], w_lo[n][:, c, h * P:(h + 1) * P],
                                           xnT_hi[:, c, :], xnT_lo[:, c, :], False, c == C - 1)
                            i.then_inc(qk_psum, 1)

                    def route_logits(g):
                        pe.wait_ge(xn2_ready, g + 1)
                        for c in range(C):
                            for t in range(T):
                                i = pe.transpose(bank[2 + c][:, t * P:(t + 1) * P], rows[:, t, c * P:(c + 1) * P], ident[:])
                            i.then_inc(xn2T_psum, 1)
                        pe.wait_ge(xn2T_ready, 2 * g + 2)
                        for t in range(T):
                            for c in range(C):
                                i = pe.matmul(bank[0][:, t * E:(t + 1) * E], xn2T[:, c, t * P:(t + 1) * P], router_t[:, c, :],
                                              start=(c == 0), stop=(c == C - 1))
                        i.then_inc(logits_psum, 1)

                    def route_ranks(g):
                        pe.wait_ge(chosen_ready, g + 1)
                        for t in range(T + 1):
                            dst = bank[1][:, t * E:(t + 1) * E]
                            if t < T:
                                i = pe.matmul(dst, before[:], chosen_bf[:, t, :], start=True, stop=(t == 0))
                            for s in range(t):
                                i = pe.matmul(dst, ones_bf[:], chosen_bf[:, s, :], start=(t == T and s == 0), stop=(s == t - 1))
                        i.then_inc(rank_psum, 1)

                    xnT(0)
                    pe.wait_ge(xnT_hi_ready, 2)
                    pe.wait_ge(xnT_lo_ready, 2)
                    for u in range(2 * C):
                        n, h = "qk"[u // C], u % C
                        dst = bank[(2 + u) % 4][:]
                        pe.matmul(dst, bias[n][:, h * P:(h + 1) * P], ones[:], start=True, stop=False)
                        for c in range(C):
                            i = split3(dst, w_hi[n][:, c, h * P:(h + 1) * P], w_lo[n][:, c, h * P:(h + 1) * P],
                                       xnT_hi[:, c, :], xnT_lo[:, c, :], False, c == C - 1)
                        i.then_inc(qk_psum, 1)

                    def graph(g, first=False, last=False):
                        pe.wait_ge(qk_hi_ready, 4 * g + 4)
                        pe.wait_ge(qk_lo_ready, 4 * g + 4)
                        for t in range(T):
                            if not first:
                                pe.wait_ge(probT_lo_ready, 4 * g - 3 + t)
                            for c in range(C):
                                i = split3(bank[4 + t][:], qk_hi[:, c, t * P:(t + 1) * P], qk_lo[:, c, t * P:(t + 1) * P],
                                           qk_hi[:, C + c, :], qk_lo[:, C + c, :], c == 0, c == C - 1)
                            i.then_inc(score_psum, 1)
                        for i2 in range(2):
                            for j in range(2):
                                t = 2 * i2 + j
                                dst = bank[i2][:, j * D:(j + 1) * D]
                                pe.matmul(dst, ones[:, 0:P], bias["v"][:], start=True, stop=False)
                                for c in range(C):
                                    i = split3(dst, xnT_hi[:, c, t * P:(t + 1) * P], xnT_lo[:, c, t * P:(t + 1) * P],
                                               w_hi["v"][:, c, :], w_lo["v"][:, c, :], False, c == C - 1)
                            i.then_inc(v_psum, 1)
                        if not first:
                            pe.wait_ge(y_ready, 4 * g)
                            pe.wait_ge(v_lo_ready, 2 * g + 2)
                            route_logits(g - 1)
                        if not last:
                            xnT(g + 1)
                        if not first:
                            route_ranks(g - 1)
                        pe.wait_ge(prob_ready, 4 * g + 4)
                        for m in range(T):
                            for t in range(T):
                                i = pe.transpose(bank[4 + m][:, t * P:(t + 1) * P], prob[:, t, m * P:(m + 1) * P], ident[:])
                            i.then_inc(probT_psum, 1)
                        pe.wait_ge(v_lo_ready, 2 * g + 2)
                        if not first:
                            pe.wait_ge(slots_ready, g)
                        for m in range(T):
                            pe.wait_ge(probT_hi_ready, 4 * g + m + 1)
                            pe.wait_ge(probT_lo_ready, 4 * g + m + 1)
                            for c in range(C):
                                i = split3(bank[c][:], v_hi[:, m, c * P:(c + 1) * P], v_lo[:, m, c * P:(c + 1) * P],
                                           probT_hi[:, m, :], probT_lo[:, m, :], m == 0, m == T - 1)
                                if m == T - 1:
                                    i.then_inc(o_psum, 1)
                        if not last:
                            qk(g + 1)
                            pe.wait_ge(qk_lo_ready, 4 * g + 6)
                        else:
                            pe.wait_ge(xn2T_ready, 2 * g)
                        pe.wait_ge(o_hi_ready, 2 * g + 2)
                        pe.wait_ge(o_lo_ready, 2 * g + 2)
                        for i2 in range(2):
                            for j in range(2):
                                t = 2 * i2 + j
                                dst = bank[2 + i2][:, j * D:(j + 1) * D]
                                for c in range(C):
                                    i = split3(dst, oT_hi[:, c, t * P:(t + 1) * P], oT_lo[:, c, t * P:(t + 1) * P],
                                               w_hi["o"][:, c, :], w_lo["o"][:, c, :], c == 0, c == C - 1)
                            i.then_inc(y_psum, 1)

                    graph(0, first=True)
                    with pe.Fori(1, G - 1) as g:
                        graph(g)
                    graph(G - 1, last=True)
                    pe.wait_ge(y_ready, 4 * G)
                    route_logits(G - 1)
                    route_ranks(G - 1)

        with ExitStack() as ph:
            MAT = C * D
            WCOLS = 4 * MAT + D
            experts = sb(ph, "experts", [P, E, WCOLS], F32R)
            b1_all = sb(ph, "b1_all", [P, E, C], F32)
            now = sb(ph, "now", [P, 2, WCOLS], F32R)
            b1_now = sb(ph, "b1_now", [P, 2, C], F32)
            stage = sb(ph, "stage", [P, 4, MAT], F32)
            b2_stage = sb(ph, "b2_stage", [P, 2, D], F32)
            b1_rows = sb(ph, "b1_rows", [E, D], F32)
            pad = sb(ph, "pad", [P, T, ROW], F32)
            pad_id = sb(ph, "pad_id", [P, T], F32)

            table = sb(ph, "table", [P, 8, E], F32)
            table_i = sb(ph, "table_i", [P, 2, E], I32)
            block_no = sb(ph, "block_no", [P, NBLOCKS], F32)
            block_at = sb(ph, "block_at", [P, NBLOCKS], F32)
            block_e = sb(ph, "block_e", [P, 4, NBLOCKS], F32)
            ended = sb(ph, "ended", [P, NBLOCKS, E], F32)
            inside = sb(ph, "inside", [P, NBLOCKS, E], F32)
            start_of = sb(ph, "start_of", [P, NBLOCKS, E], F32)
            first_row = sb(ph, "first_row", [P, NBLOCKS], I32)
            expert_of = sb(ph, "expert_of", [P, NBLOCKS], I32)

            xrow = sb(ph, "xrow", [P, 2, T, ROW], F32)
            token = sb(ph, "token", [P, 2, T], U32)
            gate = sb(ph, "gate", [P, 2, T], F32)
            xT_hi = sb(ph, "xT_hi", [P, C, BLOCK], F32R)
            xT_lo = sb(ph, "xT_lo", [P, C, BLOCK], F32R)
            h_sb = sb(ph, "h_sb", [P, C, BLOCK], F32)
            h_hi = sb(ph, "h_hi", [P, C, BLOCK], F32R)
            h_lo = sb(ph, "h_lo", [P, C, BLOCK], F32R)
            y = sb(ph, "y", [P, 2, T, D], F32)

            expert_loaded = [sem(f"expert_loaded{i}") for i in range(4)]
            b2_loaded = [sem(f"b2_loaded{i}") for i in range(2)]
            b1_loaded = sem("b1_loaded")
            b2_zeroed = sem("b2_zeroed")
            b1_psum = sem("b1_psum")
            b1_made = sem("b1_made")
            experts_hi = sem("experts_hi")
            experts_lo = sem("experts_lo")
            pad_step = sem("pad_step")
            pad_made = sem("pad_made")
            table_step = sem("table_step")
            tables_made = sem("tables_made")
            xrow_loaded = [sem(f"xrow_loaded{q}") for q in range(2)]
            picked = sem("picked")
            now_ready = sem("now_ready")
            xT_psum = sem("xT_psum")
            xT_hi_done = sem("xT_hi_done")
            xT_lo_done = sem("xT_lo_done")
            h_psum = sem("h_psum")
            h_ready = sem("h_ready")
            h_hi_done = sem("h_hi_done")
            h_lo_done = sem("h_lo_done")
            ye_psum = sem("ye_psum")
            ye_ready = sem("ye_ready")
            added = sem("added")

            with nc.Block() as block:

                @block.sync
                def _(sp):
                    for e in range(E):
                        for m, w in enumerate((w1, w2)):
                            s = (2 * e + m) % 4
                            if e >= 2:
                                sp.wait_ge(experts_lo, 3 * (e - 2) + m + 1)
                            sp.dma_start(stage[:, s, :].rearrange("p (c n) -> p c n", c=C),
                                         w[e].rearrange("(c p) n -> p c n", p=P)).then_inc(expert_loaded[s], 16)
                        sp.wait_ge(b2_zeroed, 1)
                        if e >= 2:
                            sp.wait_ge(experts_lo, 3 * (e - 2) + 3)
                        for row in (0, 32):
                            sp.dma_start(b2_stage[row:row + 1, e % 2, :], b2[e:e + 1, :]).then_inc(b2_loaded[e % 2], 16)
                        if e == 0:
                            sp.dma_start(b1_rows[:], b1).then_inc(b1_loaded, 16)
                    sp.wait_ge(pad_made, 1)
                    sp.wait_ge(tables_made, 1)
                    sp.dma_start(out_v[G * P:(G + 1) * P, :].rearrange("p (t d) -> p t d", t=T),
                                 pad[:, :, 0:D]).then_inc(pad_stored, 16)
                    sp.dma_start(rows_dram[DUMMY:DUMMY + BLOCK, :].rearrange("(p t) r -> p (t r)", t=T),
                                 pad[:].rearrange("p t r -> p (t r)")).then_inc(pad_stored, 16)
                    for e in range(E):
                        at = sp.value_load(table_i[0:1, 1, e:e + 1], min_val=0, max_val=DUMMY - BLOCK)
                        sp.dma_start(rows_dram[bass.ds(at, BLOCK), :].rearrange("(p t) r -> p (t r)", t=T),
                                     pad[:].rearrange("p t r -> p (t r)")).then_inc(pad_stored, 16)
                    sp.wait_ge(pad_stored, 16 * (E + 2))

                    def load_rows(j, q, first=False):
                        at = sp.value_load(first_row[0:1, bass.ds(j, 1)], min_val=0, max_val=DUMMY)
                        if not first:
                            wait_apart(sp, xT_psum, 2 * j - 2)
                            wait_apart(sp, picked, j - 1)
                        sp.dma_start(xrow[:, q].rearrange("p t r -> p (t r)"),
                                     rows_dram[bass.ds(at, BLOCK), :].rearrange("(p t) r -> p (t r)", t=T)).then_inc(xrow_loaded[q], 16)

                    load_rows(0, 0, True)
                    load_rows(1, 1, True)
                    with sp.Fori(1, (NBLOCKS - 1) // 2) as i:
                        load_rows(2 * i, 0)
                        load_rows(2 * i + 1, 1)
                    load_rows(NBLOCKS - 1, 0)

                @block.gpsimd
                def _(pool):
                    for s in range(2):
                        z = pool.memset(b2_stage[:, s, :], 0.0)
                    z.then_inc(b2_zeroed, 1)
                    pool.memset(pad[:], 0.0).then_inc(pad_step, 1)
                    pool.iota(pad_id[:], [[1, T]], TOKENS, T, allow_small_or_imprecise_dtypes=True).then_inc(pad_step, 1)
                    pool.iota(block_no[:], [[1, NBLOCKS]], 0, 0, allow_small_or_imprecise_dtypes=True).then_inc(pad_step, 1)
                    pool.wait_ge(pad_step, 3)
                    pool.tensor_copy(pad[:, :, ID].bitcast(U32), pad_id[:]).then_inc(pad_made, 1)

                    def add_rows(j, q, first=False):
                        if not first:
                            wait_apart(pool, added, 16 * T * j)
                        wait_apart(pool, picked, j + 1)
                        wait_apart(pool, ye_ready, 2 * j + 2)
                        for t in range(T):
                            pool.indirect_dma_start(out, bass.IndirectOffsetOnAxis(ap=token[:, q, t:t + 1], axis=0),
                                                    y[:, q, t, :], None, compute_op=ALU.add).then_inc(added, 16)

                    add_rows(0, 0, True)
                    add_rows(1, 1)
                    with pool.Fori(1, (NBLOCKS - 1) // 2) as i:
                        add_rows(2 * i, 0)
                        add_rows(2 * i + 1, 1)
                    add_rows(NBLOCKS - 1, 0)
                    pool.wait_ge(added, 16 * T * NBLOCKS)

                @block.scalar
                def _(act):
                    for e in range(E):
                        for m in range(2):
                            s = (2 * e + m) % 4
                            act.wait_ge(expert_loaded[s], 16 * (e // 2 + 1))
                            act.copy(experts[:, e, 2 * m * MAT:(2 * m + 1) * MAT], stage[:, s, :]).then_inc(experts_hi, 1)
                        act.wait_ge(b2_loaded[e % 2], 32 * (e // 2 + 1))
                        act.copy(experts[:, e, 4 * MAT:], b2_stage[:, e % 2, :]).then_inc(experts_hi, 1)

                    def x_hi(j):
                        for c in range(C):
                            act.wait_ge(xT_psum, 2 * j + c + 1)
                            act.copy(xT_hi[:, c, :], bank[c][:]).then_inc(xT_hi_done, 1)

                    def hidden(j, q, first=False):
                        act.wait_ge(now_ready, j + 1)
                        if not first:
                            act.wait_ge(h_lo_done, 2 * j)
                        for c in range(C):
                            act.wait_ge(h_psum, 2 * j + c + 1)
                            act.activation(h_sb[:, c, :], bank[2 + c][:], ACT.Gelu, bias=b1_now[:, q, c:c + 1]).then_inc(h_ready, 1)

                    def weigh(j, q, first=False):
                        act.wait_ge(picked, j + 1)
                        if not first:
                            act.wait_ge(added, 16 * T * (j - 1))
                        for i in range(2):
                            act.wait_ge(ye_psum, 2 * j + i + 1)
                            for t in (2 * i, 2 * i + 1):
                                k = act.activation(y[:, q, t, :], bank[4 + i][:, (t % 2) * D:(t % 2 + 1) * D], ACT.Copy,
                                                   scale=gate[:, q, t:t + 1])
                            k.then_inc(ye_ready, 1)

                    x_hi(0)
                    hidden(0, 0, True)
                    x_hi(1)
                    weigh(0, 0, True)
                    hidden(1, 1)
                    x_hi(2)
                    weigh(1, 1, True)
                    with act.Fori(1, (NBLOCKS - 1) // 2) as i:
                        for q in range(2):
                            hidden(2 * i + q, q)
                            x_hi(2 * i + q + 1)
                            weigh(2 * i + q, q)
                    hidden(NBLOCKS - 1, 0)
                    weigh(NBLOCKS - 1, 0)

                @block.vector
                def _(dve):
                    step = [0]

                    def then(i):
                        step[0] += 1
                        i.then_inc(table_step, 1)
                        dve.wait_ge(table_step, step[0])

                    def over_blocks(ap):
                        return ap.unsqueeze(1).to_broadcast([P, NBLOCKS, E])

                    def over_experts(ap):
                        return ap.unsqueeze(2).to_broadcast([P, NBLOCKS, E])

                    REGION0, COUNT, BLOCKS, END, START = range(5)
                    dve.wait_ge(pad_made, 1)
                    then(dve.tensor_scalar(table[:, REGION0, :], expert_no[:], float(REGION), None, ALU.mult))
                    then(dve.tensor_tensor(table[:, COUNT, :], carry[:], table[:, REGION0, :], ALU.subtract))
                    then(dve.tensor_scalar(table_i[:, 0, :], table[:, COUNT, :], float(BLOCK - 1), None, ALU.add))
                    then(dve.tensor_scalar(table_i[:, 1, :], table_i[:, 0, :], 9, None, ALU.logical_shift_right))
                    then(dve.tensor_copy(table[:, BLOCKS, :], table_i[:, 1, :]))
                    then(dve.tensor_copy(table[:, END, :], table[:, BLOCKS, :]))
                    for e in range(1, E):
                        then(dve.tensor_tensor(table[:, END, e:e + 1], table[:, END, e - 1:e], table[:, BLOCKS, e:e + 1], ALU.add))
                    then(dve.tensor_tensor(table[:, START, :], table[:, END, :], table[:, BLOCKS, :], ALU.subtract))
                    then(dve.scalar_tensor_tensor(table[:, START, :], table[:, START, :], -float(BLOCK), table[:, REGION0, :],
                                                  ALU.mult, ALU.add))
                    then(dve.tensor_copy(table_i[:, 1, :], carry[:]))
                    then(dve.tensor_tensor(ended[:], over_experts(block_no[:]), over_blocks(table[:, END, :]), ALU.is_ge))
                    dve.tensor_scalar(inside[:, :, 0:1], ended[:, :, 0:1], -1.0, 1.0, ALU.mult, ALU.add)
                    then(dve.tensor_tensor(inside[:, :, 1:E], ended[:, :, 0:E - 1], ended[:, :, 1:E], ALU.subtract))
                    then(dve.tensor_scalar(block_at[:], block_no[:], float(BLOCK), float(-DUMMY), ALU.mult, ALU.add))
                    then(dve.tensor_tensor(start_of[:], over_experts(block_at[:]), over_blocks(table[:, START, :]), ALU.add))
                    then(dve.tensor_tensor(start_of[:], start_of[:], inside[:], ALU.mult))
                    then(dve.tensor_reduce(block_e[:, 0, :], start_of[:], AX.X, ALU.add))
                    then(dve.tensor_scalar(first_row[:], block_e[:, 0, :], float(DUMMY), None, ALU.add))
                    then(dve.tensor_reduce(block_e[:, 1, :], ended[:], AX.X, ALU.add))
                    then(dve.tensor_scalar(expert_of[:], block_e[:, 1, :], float(E - 1), None, ALU.min))
                    dve.sem_inc(tables_made, 1)

                    for e in range(E):
                        for m in range(2):
                            dve.wait_ge(experts_hi, 3 * e + m + 1)
                            dve.tensor_tensor(experts[:, e, (2 * m + 1) * MAT:(2 * m + 2) * MAT], stage[:, (2 * e + m) % 4, :],
                                              experts[:, e, 2 * m * MAT:(2 * m + 1) * MAT].bitcast(F32),
                                              ALU.subtract).then_inc(experts_lo, 1)
                        dve.wait_ge(experts_hi, 3 * e + 3)
                        dve.tensor_tensor(experts[32:33, e, 4 * MAT:], b2_stage[32:33, e % 2, :],
                                          experts[32:33, e, 4 * MAT:].bitcast(F32), ALU.subtract).then_inc(experts_lo, 1)
                    dve.wait_ge(b1_psum, 1)
                    dve.tensor_copy(b1_all[:], bank[7][:, 0:C * E].rearrange("p (c e) -> p e c", c=C)).then_inc(b1_made, 1)
                    dve.wait_ge(b1_made, 1)
                    dve.wait_ge(experts_lo, 3 * E)

                    def pick(j, q, pair, first=False):
                        e = dve.value_load(expert_of[0:1, bass.ds(j, 1)], min_val=0, max_val=E - 1)
                        if not first:
                            dve.wait_ge(ye_psum, 2 * j - 2)
                            dve.wait_ge(h_ready, 2 * j - 2)
                        dve.tensor_copy(b1_now[:, q], b1_all[:, bass.ds(e, 1), :].rearrange("p o c -> p (o c)"))
                        dve.tensor_copy(now[:, q], experts[:, bass.ds(e, 1), :].rearrange("p o c -> p (o c)")).then_inc(now_ready, 1)
                        dve.wait_ge(xrow_loaded[q], 16 * pair + 16)
                        if not first:
                            dve.wait_ge(added, 16 * T * (j - 1))
                            dve.wait_ge(ye_ready, 2 * j - 2)
                        dve.tensor_copy(token[:, q], xrow[:, q, :, ID].bitcast(U32))
                        dve.tensor_copy(gate[:, q], xrow[:, q, :, bass.ds(e + GATE, 1)].rearrange("p t o -> p (t o)")).then_inc(picked, 1)

                    def x_lo(j):
                        for c in range(C):
                            dve.wait_ge(xT_hi_done, 2 * j + c + 1)
                            dve.tensor_tensor(xT_lo[:, c, :], bank[c][:], xT_hi[:, c, :].bitcast(F32),
                                              ALU.subtract).then_inc(xT_lo_done, 1)

                    def split_hidden(j, first=False):
                        if not first:
                            dve.wait_ge(ye_psum, 2 * j)
                        for c in range(C):
                            dve.wait_ge(h_ready, 2 * j + c + 1)
                            dve.tensor_copy(h_hi[:, c, :], h_sb[:, c, :]).then_inc(h_hi_done, 1)
                        for c in range(C):
                            dve.wait_ge(h_hi_done, 2 * j + c + 1)
                            dve.tensor_tensor(h_lo[:, c, :], h_sb[:, c, :], h_hi[:, c, :].bitcast(F32),
                                              ALU.subtract).then_inc(h_lo_done, 1)

                    pick(0, 0, 0, True)
                    x_lo(0)
                    pick(1, 1, 0, True)
                    split_hidden(0, True)
                    x_lo(1)
                    pick(2, 0, 1)
                    split_hidden(1)
                    x_lo(2)
                    with dve.Fori(1, (NBLOCKS - 1) // 2) as i:
                        for q in range(2):
                            pick(2 * i + q + 1, 1 - q, i + q)
                            split_hidden(2 * i + q)
                            x_lo(2 * i + q + 1)
                    split_hidden(NBLOCKS - 1)

                @block.tensor
                def _(pe):
                    pe.wait_ge(b1_loaded, 16)
                    for c in range(C):
                        i = pe.transpose(bank[7][:, c * E:(c + 1) * E], b1_rows[:, c * P:(c + 1) * P], ident[0:E, 0:E])
                    i.then_inc(b1_psum, 1)

                    def split3(dst, a_hi, a_lo, b_hi, b_lo, start, stop):
                        pe.matmul(dst, a_hi, b_hi, start=start, stop=False)
                        pe.matmul(dst, a_hi, b_lo, start=False, stop=False)
                        return pe.matmul(dst, a_lo, b_hi, start=False, stop=stop)

                    def mat(q, which, c):
                        return now[:, q, which * MAT + c * D:which * MAT + (c + 1) * D]

                    def turn(j, q, pair, first=False):
                        pe.wait_ge(xrow_loaded[q], 16 * pair + 16)
                        if not first:
                            pe.wait_ge(xT_lo_done, 2 * j)
                        for c in range(C):
                            for t in range(T):
                                i = pe.transpose(bank[c][:, t * P:(t + 1) * P], xrow[:, q, t, c * P:(c + 1) * P], ident[:])
                            i.then_inc(xT_psum, 1)

                    def layer1(j, q, first=False):
                        pe.wait_ge(now_ready, j + 1)
                        pe.wait_ge(xT_hi_done, 2 * j + 2)
                        pe.wait_ge(xT_lo_done, 2 * j + 2)
                        if not first:
                            pe.wait_ge(h_ready, 2 * j)
                        for h in range(C):
                            for c in range(C):
                                i = split3(bank[2 + h][:], mat(q, 0, c)[:, h * P:(h + 1) * P], mat(q, 1, c)[:, h * P:(h + 1) * P],
                                           xT_hi[:, c, :], xT_lo[:, c, :], c == 0, c == C - 1)
                            i.then_inc(h_psum, 1)

                    def layer2(j, q, first=False):
                        pe.wait_ge(h_hi_done, 2 * j + 2)
                        pe.wait_ge(h_lo_done, 2 * j + 2)
                        if not first:
                            pe.wait_ge(ye_ready, 2 * j)
                        for i2 in range(2):
                            for t in (2 * i2, 2 * i2 + 1):
                                dst = bank[4 + i2][:, (t % 2) * D:(t % 2 + 1) * D]
                                pe.matmul(dst, ones[:, 0:P], now[:, q, 4 * MAT:], start=True, stop=False)
                                for c in range(C):
                                    i = split3(dst, h_hi[:, c, t * P:(t + 1) * P], h_lo[:, c, t * P:(t + 1) * P],
                                               mat(q, 2, c), mat(q, 3, c), False, c == C - 1)
                            i.then_inc(ye_psum, 1)

                    turn(0, 0, 0, True)
                    layer1(0, 0, True)
                    turn(1, 1, 0)
                    layer2(0, 0, True)
                    layer1(1, 1)
                    turn(2, 0, 1)
                    layer2(1, 1)
                    with pe.Fori(1, (NBLOCKS - 1) // 2) as i:
                        for q in range(2):
                            layer1(2 * i + q, q)
                            turn(2 * i + q + 1, 1 - q, i + q)
                            layer2(2 * i + q, q)
                    layer1(NBLOCKS - 1, 0)
                    layer2(NBLOCKS - 1, 0)


_INS = ["x", "adj", "L0_gnn_Wv", "L0_gnn_bv", "L0_gnn_Wk", "L0_gnn_bk", "L0_gnn_Wq", "L0_gnn_bq", "L0_gnn_Wo",
        "L0_gnn_bo", "L0_ffn_router_w", "L0_ffn_w1", "L0_ffn_b1", "L0_ffn_w2", "L0_ffn_b2"]


def kernel(**inputs):
    import numpy as np
    import concourse.bacc as bacc
    from concourse.bass_utils import run_bass_kernel_spmd

    nc = bacc.Bacc("TRN2", target_bir_lowering=False, num_devices=1)
    arrays, args = {}, []
    for name in _INS:
        a = np.ascontiguousarray(inputs[name])
        arrays[f"in_{name}"] = a
        args.append(nc.dram_tensor(f"in_{name}", a.shape, mybir.dt.from_np(a.dtype), kind="ExternalInput").ap())
    g, n, d = inputs["x"].shape
    args.append(nc.dram_tensor("out_rows", [g * n + 512, d], F32, kind="ExternalOutput").ap())
    build_program(nc, *args)
    r = run_bass_kernel_spmd(nc, [arrays], core_ids=[0])
    return r.results[0]["out_rows"][:g * n].reshape(g, n, d)
```

```python
from contextlib import ExitStack

import concourse.bass as bass
from concourse import mybir

P = 128
F32 = mybir.dt.float32
F32R = mybir.dt.float32r
BF16 = mybir.dt.bfloat16
U32 = mybir.dt.uint32
I32 = mybir.dt.int32
ALU = mybir.AluOpType
ACT = mybir.ActivationFunctionType
AX = mybir.AxisListType

NEG = 9000000000000000.0
EPS = 1e-5
BIG = 3.0e38


def build_program(nc, x, adj, wv, bv, wk, bk, wq, bq, wo, bo, router_w, w1, b1, w2, b2, out):
    G, N, D = x.shape
    E = router_w.shape[0]
    T = N // P
    C = D // P
    TOKENS = G * N
    BLOCK = 512
    REGION = TOKENS + BLOCK
    DUMMY = E * REGION
    NBLOCKS = (2 * TOKENS + E * (BLOCK - 1)) // BLOCK
    ID = D
    GATE = D + 1
    ROW = 272
    assert GATE + E <= ROW and N == BLOCK == 4 * P and D == 2 * P

    rows_dram = nc.dram_tensor("rows_dram", [DUMMY + BLOCK, ROW], F32, kind="Internal").ap()

    x_v = x.rearrange("g (p t) d -> (g p) (t d)", t=T)
    adj_v = adj.rearrange("g (p t) m -> (g p) (t m)", t=T)
    out_v = out.rearrange("(q t) d -> q (t d)", t=T)

    with ExitStack() as whole:
        def sb(stack, name, shape, dt):
            return stack.enter_context(nc.sbuf_tensor(name, shape, dt))

        def sem(name):
            return whole.enter_context(nc.semaphore(name))

        bank = [whole.enter_context(nc.psum_tensor(f"bank{i}", [P, 512], F32)) for i in range(8)]

        ident = sb(whole, "ident", [P, P], F32)
        ones = sb(whole, "ones", [P, 512], F32R)
        before = sb(whole, "before", [P, P], BF16)
        ones_bf = sb(whole, "ones_bf", [P, P], BF16)
        expert_no = sb(whole, "expert_no", [P, E], F32)
        carry = sb(whole, "carry", [P, E], F32)

        loaded = sem("loaded")
        waited_apart = sem("waited_apart")
        consts_made = sem("consts_made")

        def wait_apart(eng, what, value):
            eng.wait_ge(what, value)
            eng.sem_inc(waited_apart, 1)

        with ExitStack() as ph:
            w_hi = {n: sb(ph, f"w{n}_hi", [P, C, D], F32R) for n in "qkvo"}
            w_lo = {n: sb(ph, f"w{n}_lo", [P, C, D], F32R) for n in "qkvo"}
            bias = {n: sb(ph, f"bias_{n}", [P, D], F32R) for n in "qkv"}
            bo_rows = sb(ph, "bo_rows", [P, D], F32)
            router_rows = sb(ph, "router_rows", [E, D], F32)
            router_t = sb(ph, "router_t", [P, C, E], F32)
            minus_half = sb(ph, "minus_half", [P, T], F32)
            id_f = sb(ph, "id_f", [P, T], F32)

            x_norm = sb(ph, "x_norm", [P, T, D], F32)
            x_res = sb(ph, "x_res", [P, T, D], F32)
            adj_t = sb(ph, "adj_t", [P, T, N], F32)
            neg_mask = sb(ph, "neg_mask", [P, T, N], F32)
            xn = sb(ph, "xn", [P, T, D], F32)
            xnT_hi = sb(ph, "xnT_hi", [P, C, N], F32R)
            xnT_lo = sb(ph, "xnT_lo", [P, C, N], F32R)
            qk_hi = sb(ph, "qk_hi", [P, 2 * C, N], F32R)
            qk_lo = sb(ph, "qk_lo", [P, 2 * C, N], F32R)
            v_hi = sb(ph, "v_hi", [P, T, D], F32R)
            v_lo = sb(ph, "v_lo", [P, T, D], F32R)
            prob = sb(ph, "prob", [P, T, N], F32)
            probT_hi = sb(ph, "probT_hi", [P, T, N], F32R)
            probT_lo = sb(ph, "probT_lo", [P, T, N], F32R)
            oT_hi = sb(ph, "oT_hi", [P, C, N], F32R)
            oT_lo = sb(ph, "oT_lo", [P, C, N], F32R)
            y_sb = sb(ph, "y_sb", [P, T, D], F32)
            x1 = sb(ph, "x1", [P, T, D], F32)
            rows = sb(ph, "rows", [P, T, ROW], F32)
            xn2T = sb(ph, "xn2T", [P, C, N], F32)

            neg_max = sb(ph, "neg_max", [P, T], F32)
            row_sum = sb(ph, "row_sum", [P, T], F32)
            row_inv = sb(ph, "row_inv", [P, T], F32)
            st = {n: sb(ph, f"st{n}", [P, T, 6], F32) for n in "12"}
            mv = {n: sb(ph, f"mv{n}", [P, T, 2], F32) for n in "12"}
            var_eps = {n: sb(ph, f"var_eps{n}", [P, T], F32) for n in "12"}
            neg_mean = {n: sb(ph, f"neg_mean{n}", [P, T], F32) for n in "12"}
            rstd = {n: sb(ph, f"rstd{n}", [P, T], F32) for n in "12"}
            norm_bias = {n: sb(ph, f"norm_bias{n}", [P, T], F32) for n in "12"}

            logitsT = sb(ph, "logitsT", [E, N], F32)
            logits = sb(ph, "logits", [P, T, E], F32)
            top8 = sb(ph, "top8", [P, T, 8], F32)
            top8_at = sb(ph, "top8_at", [P, T, 8], U32)
            top2_at = sb(ph, "top2_at", [P, T, 2], F32)
            is_top = sb(ph, "is_top", [P, 2, T, E], F32)
            chosen = sb(ph, "chosen", [P, T, E], F32)
            chosen_bf = sb(ph, "chosen_bf", [P, T, E], BF16)
            shifted = sb(ph, "shifted", [P, T, E], F32)
            expo = sb(ph, "expo", [P, T, E], F32)
            gate_sum = sb(ph, "gate_sum", [P, 4, T], F32)
            gates = sb(ph, "gates", [P, 2, T, E], F32)
            place = sb(ph, "place", [P, T, E], F32)
            place_top = sb(ph, "place_top", [P, 2, T, E], F32)
            slot_f = sb(ph, "slot_f", [P, 2, T], F32)
            slot = sb(ph, "slot", [P, 2, T], U32)

            xnorm_loaded = sem("xnorm_loaded")
            xres_loaded = sem("xres_loaded")
            adj_loaded = sem("adj_loaded")
            var_ready = {n: sem(f"var{n}_ready") for n in "12"}
            rstd_ready = {n: sem(f"rstd{n}_ready") for n in "12"}
            root_step = {n: sem(f"root{n}_step") for n in "12"}
            stats_step = {n: sem(f"stats{n}_step") for n in "12"}
            xn_ready = sem("xn_ready")
            xnT_psum = sem("xnT_psum")
            xnT_hi_ready = sem("xnT_hi_ready")
            xnT_lo_ready = sem("xnT_lo_ready")
            qk_psum = sem("qk_psum")
            qk_hi_ready = sem("qk_hi_ready")
            qk_lo_ready = sem("qk_lo_ready")
            v_psum = sem("v_psum")
            v_hi_ready = sem("v_hi_ready")
            v_lo_ready = sem("v_lo_ready")
            score_psum = sem("score_psum")
            negmask_ready = sem("negmask_ready")
            masked = sem("masked")
            shift_ready = sem("shift_ready")
            prob_ready = sem("prob_ready")
            probT_psum = sem("probT_psum")
            probT_hi_ready = sem("probT_hi_ready")
            probT_lo_ready = sem("probT_lo_ready")
            o_psum = sem("o_psum")
            o_hi_ready = sem("o_hi_ready")
            o_lo_ready = sem("o_lo_ready")
            inv_ready = sem("inv_ready")
            y_psum = sem("y_psum")
            y_ready = sem("y_ready")
            x1_ready = sem("x1_ready")
            xn2_ready = sem("xn2_ready")
            base_ready = sem("base_ready")
            base_stored = sem("base_stored")
            xn2T_psum = sem("xn2T_psum")
            xn2T_ready = sem("xn2T_ready")
            logitsT_psum = sem("logitsT_psum")
            logitsT_ready = sem("logitsT_ready")
            logits_psum = sem("logits_psum")
            expo_in = sem("expo_in")
            expo_ready = sem("expo_ready")
            chosen_ready = sem("chosen_ready")
            rank_psum = sem("rank_psum")
            gates_ready = sem("gates_ready")
            slots_ready = sem("slots_ready")
            id_ready = sem("id_ready")
            id_step = sem("id_step")
            scattered = sem("scattered")
            route_step = sem("route_step")
            ROUTE = 16
            hi_made = sem("hi_made")
            lo_made = sem("lo_made")
            bias_zeroed = sem("bias_zeroed")
            router_psum = sem("router_psum")
            router_made = sem("router_made")
            pool_step = sem("pool_step")
            pad_stored = sem("pad_stored")

            with nc.Block() as block:
                w_stage = {"q": prob[:, 0, :], "k": prob[:, 1, :], "v": prob[:, 2, :], "o": prob[:, 3, :]}
                b_stage = {"q": y_sb[:, 0, :], "k": y_sb[:, 1, :], "v": y_sb[:, 2, :]}
                w_in = {"q": wq, "k": wk, "v": wv, "o": wo}
                b_in = {"q": bq, "k": bk, "v": bv}
                SETUP_LOADS = 4 + 6 + 2

                @block.sync
                def _(sp):
                    for n in "qkvo":
                        sp.dma_start(w_stage[n].rearrange("p (c n) -> p c n", c=C),
                                     w_in[n].rearrange("(c p) n -> p c n", p=P)).then_inc(loaded, 16)
                    sp.wait_ge(bias_zeroed, 1)
                    for n in "qkv":
                        for row in (0, 32):
                            sp.dma_start(b_stage[n][row:row + 1, :], b_in[n].rearrange("(o n) -> o n", o=1)).then_inc(loaded, 16)
                    sp.dma_start(bo_rows[:], bo.partition_broadcast(P)).then_inc(loaded, 16)
                    sp.dma_start(router_rows[:], router_w).then_inc(loaded, 16)
                    sp.dma_start(x_norm[:].rearrange("p t d -> p (t d)"), x_v[0:P, :]).then_inc(xnorm_loaded, 16)
                    sp.dma_start(x_res[:].rearrange("p t d -> p (t d)"), x_v[0:P, :]).then_inc(xres_loaded, 16)
                    sp.dma_start(adj_t[:].rearrange("p t m -> p (t m)"), adj_v[0:P, :]).then_inc(adj_loaded, 16)
                    sp.wait_ge(xn_ready, 1)
                    sp.dma_start(x_norm[:].rearrange("p t d -> p (t d)"), x_v[P:2 * P, :]).then_inc(xnorm_loaded, 16)

                    def graph(g, first=False, load_next=True, load_after=True):
                        if load_after:
                            wait_apart(sp, xn_ready, g + 2)
                            sp.dma_start(x_norm[:].rearrange("p t d -> p (t d)"),
                                         x_v[bass.ds(g * P + 2 * P, P), :]).then_inc(xnorm_loaded, 16)
                        if load_next:
                            wait_apart(sp, masked, 4 * g + 4)
                            wait_apart(sp, negmask_ready, g + 1)
                            sp.dma_start(adj_t[:].rearrange("p t m -> p (t m)"),
                                         adj_v[bass.ds(g * P + P, P), :]).then_inc(adj_loaded, 16)
                        if not first:
                            wait_apart(sp, base_ready, g)
                            sp.dma_start(out_v[bass.ds(g * P - P, P), :],
                                         x1[:].rearrange("p t d -> p (t d)")).then_inc(base_stored, 16)
                        if load_next:
                            wait_apart(sp, x1_ready, 2 * g + 2)
                            sp.dma_start(x_res[:].rearrange("p t d -> p (t d)"),
                                         x_v[bass.ds(g * P + P, P), :]).then_inc(xres_loaded, 16)

                    graph(0, first=True)
                    with sp.Fori(1, G - 2) as g:
                        graph(g)
                    graph(G - 2, load_after=False)
                    graph(G - 1, load_next=False, load_after=False)
                    sp.wait_ge(base_ready, G)
                    sp.dma_start(out_v[(G - 1) * P:G * P, :], x1[:].rearrange("p t d -> p (t d)")).then_inc(base_stored, 16)
                    sp.wait_ge(base_stored, 16 * G)

                @block.gpsimd
                def _(pool):
                    pool.memset(ident[:], 0.0).then_inc(pool_step, 1)
                    pool.memset(before[:], 1.0).then_inc(pool_step, 1)
                    pool.memset(ones_bf[:], 1.0)
                    pool.memset(minus_half[:], -0.5)
                    for n in "qkv":
                        z = pool.memset(b_stage[n], 0.0)
                    z.then_inc(bias_zeroed, 1)
                    pool.memset(rows[:], 0.0).then_inc(pool_step, 1)
                    pool.iota(expert_no[:], [[1, E]], 0, 0, allow_small_or_imprecise_dtypes=True)
                    pool.iota(id_f[:], [[1, T]], 0, T, allow_small_or_imprecise_dtypes=True).then_inc(pool_step, 1)
                    pool.iota(carry[:], [[1, E]], 0, 0, allow_small_or_imprecise_dtypes=True).then_inc(pool_step, 1)
                    pool.wait_ge(pool_step, 5)
                    pool.affine_select(out=ident[:], in_=ident[:], compare_op=ALU.not_equal, fill=1.0, base=0,
                                       pattern=[[-1, P]], channel_multiplier=1)
                    pool.affine_select(out=before[:], in_=before[:], compare_op=ALU.is_gt, fill=0.0, base=0,
                                       pattern=[[1, P]], channel_multiplier=-1)
                    pool.tensor_scalar(carry[:], carry[:], float(REGION), 0.0, ALU.mult, ALU.add).then_inc(consts_made, 1)

                    def neg_of_mask(g):
                        wait_apart(pool, adj_loaded, 16 * g + 16)
                        pool.tensor_scalar(neg_mask[:].rearrange("q s (t p) -> q s t p", t=T), adj_t[:].rearrange("q s (p t) -> q s t p", t=T),
                                           -NEG, NEG, ALU.mult, ALU.add).then_inc(negmask_ready, 1)

                    def root(n, g, read):
                        wait_apart(pool, var_ready[n], g + 1)
                        if not (isinstance(g, int) and g == 0):
                            pool.wait_ge(read, g)
                        pool.tensor_tensor(rstd[n][:], var_eps[n][:], minus_half[:], ALU.pow).then_inc(root_step[n], 1)
                        pool.wait_ge(root_step[n], g + 1)
                        pool.tensor_tensor(norm_bias[n][:], neg_mean[n][:], rstd[n][:], ALU.mult).then_inc(rstd_ready[n], 1)

                    def write_ids(g, first):
                        if not first:
                            wait_apart(pool, scattered, 16 * 2 * T * g)
                        pool.tensor_copy(rows[:, :, ID].bitcast(U32), id_f[:]).then_inc(id_ready, 1)
                        wait_apart(pool, id_ready, g + 1)
                        pool.tensor_scalar(id_f[:], id_f[:], 1.0, float(N), ALU.mult, ALU.add).then_inc(id_step, 1)

                    def base(g, first):
                        pool.wait_ge(x1_ready, 2 * g + 2)
                        pool.wait_ge(xn2_ready, g + 1)
                        pool.tensor_tensor(x1[:], x1[:], rows[:, :, 0:D], ALU.add).then_inc(base_ready, 1)

                    def scatter(g):
                        wait_apart(pool, id_ready, g + 1)
                        wait_apart(pool, gates_ready, g + 1)
                        wait_apart(pool, slots_ready, g + 1)
                        for t in range(T):
                            for k in range(2):
                                pool.indirect_dma_start(
                                    rows_dram, bass.IndirectOffsetOnAxis(ap=slot[:, k, t:t + 1], axis=0),
                                    rows[:, t, :], None).then_inc(scattered, 16)

                    root("1", 0, xn_ready)
                    neg_of_mask(0)
                    root("1", 1, xn_ready)

                    def graph(g, first=False, second=False, last=False, load_after=True):
                        if not first:
                            root("2", g - 1, xn2_ready)
                            write_ids(g - 1, second)
                            base(g - 1, second)
                        if load_after:
                            root("1", g + 2, xn_ready)
                        if not last:
                            wait_apart(pool, shift_ready, 4 * g + 4)
                            neg_of_mask(g + 1)
                        if not first:
                            scatter(g - 1)

                    graph(0, first=True)
                    graph(1, second=True)
                    with pool.Fori(2, G - 2) as g:
                        graph(g)
                    graph(G - 2, load_after=False)
                    graph(G - 1, last=True, load_after=False)
                    root("2", G - 1, xn2_ready)
                    write_ids(G - 1, False)
                    base(G - 1, False)
                    scatter(G - 1)
                    pool.wait_ge(scattered, 16 * 2 * T * G)

                @block.scalar
                def _(act):
                    for n in "qkvo":
                        act.wait_ge(loaded, 16 * SETUP_LOADS)
                        act.copy(w_hi[n][:].rearrange("p c n -> p (c n)"), w_stage[n]).then_inc(hi_made, 1)
                    for n in "qkv":
                        act.copy(bias[n][:], b_stage[n]).then_inc(hi_made, 1)

                    def norm(n, dst, src):
                        for t in range(T):
                            i = act.activation(dst[:, t, 0:D], src[:, t, :], ACT.Identity, bias=norm_bias[n][:, t:t + 1],
                                               scale=rstd[n][:, t:t + 1])
                        return i

                    def apply1(g, first=False):
                        act.wait_ge(rstd_ready["1"], g + 1)
                        if not first:
                            act.wait_ge(xnT_psum, 2 * g)
                        norm("1", xn, x_norm).then_inc(xn_ready, 1)

                    def apply2(g, first=False):
                        act.wait_ge(rstd_ready["2"], g + 1)
                        if not first:
                            act.wait_ge(scattered, 16 * 2 * T * g)
                        norm("2", rows, x1).then_inc(xn2_ready, 1)

                    def xnT(g):
                        for c in range(C):
                            act.wait_ge(xnT_psum, 2 * g + c + 1)
                            act.copy(xnT_hi[:, c, :], bank[2 + c][:]).then_inc(xnT_hi_ready, 1)

                    def qk(g, u):
                        act.wait_ge(qk_psum, 4 * g + u + 1)
                        act.activation(qk_hi[:, u, :], bank[4 + u][:], ACT.Relu).then_inc(qk_hi_ready, 1)

                    apply1(0, True)
                    xnT(0)
                    for u in range(2 * C):
                        qk(0, u)

                    def graph(g, first=False, second=False, last=False):
                        if not last:
                            apply1(g + 1)
                        if not first:
                            act.wait_ge(inv_ready, g)
                        for t in range(T):
                            act.wait_ge(shift_ready, 4 * g + t + 1)
                            act.activation(prob[:, t, :], prob[:, t, :], ACT.Exp, bias=neg_max[:, t:t + 1], scale=-1.0,
                                           accum_out=row_sum[:, t:t + 1]).then_inc(prob_ready, 1)
                        for i in range(2):
                            act.wait_ge(v_psum, 2 * g + i + 1)
                            act.activation(v_hi[:, 2 * i:2 * i + 2, :].rearrange("p t d -> p (t d)"), bank[i][:],
                                           ACT.Relu).then_inc(v_hi_ready, 1)
                        if not last:
                            xnT(g + 1)
                        for m in range(T):
                            act.wait_ge(probT_psum, 4 * g + m + 1)
                            act.copy(probT_hi[:, m, :], bank[4 + m][:]).then_inc(probT_hi_ready, 1)
                        if not first:
                            apply2(g - 1, second)
                        for c in range(C):
                            act.wait_ge(o_psum, 2 * g + c + 1)
                            act.copy(oT_hi[:, c, :], bank[c][:]).then_inc(o_hi_ready, 1)
                        if not first:
                            route_in(g - 1)
                        if not last:
                            qk(g + 1, 0)
                        if not first:
                            route_logits(g - 1)
                        if not last:
                            qk(g + 1, 1)
                            qk(g + 1, 2)
                        if not first:
                            route_exp(g - 1)
                        if not last:
                            qk(g + 1, 3)

                    def route_in(g):
                        for c in range(C):
                            act.wait_ge(xn2T_psum, 2 * g + c + 1)
                            act.copy(xn2T[:, c, :], bank[2 + c][:]).then_inc(xn2T_ready, 1)

                    def route_logits(g):
                        act.wait_ge(logitsT_psum, g + 1)
                        act.copy(logitsT[:], bank[2][0:E, :]).then_inc(logitsT_ready, 1)

                    def route_exp(g):
                        act.wait_ge(expo_in, g + 1)
                        act.activation(expo[:], shifted[:], ACT.Exp).then_inc(expo_ready, 1)

                    graph(0, first=True)
                    graph(1, second=True)
                    with act.Fori(2, G - 1) as g:
                        graph(g)
                    graph(G - 1, last=True)
                    apply2(G - 1)
                    route_in(G - 1)
                    route_logits(G - 1)
                    route_exp(G - 1)

                @block.vector
                def _(dve):
                    dve.wait_ge(consts_made, 1)
                    dve.memset(ones[:].bitcast(F32), 1.0)
                    dve.wait_ge(loaded, 16 * SETUP_LOADS)
                    for i, n in enumerate("qkvo"):
                        dve.wait_ge(hi_made, i + 1)
                        dve.tensor_tensor(w_lo[n][:].rearrange("p c n -> p (c n)"), w_stage[n],
                                          w_hi[n][:].bitcast(F32).rearrange("p c n -> p (c n)"), ALU.subtract).then_inc(lo_made, 1)
                    dve.wait_ge(hi_made, 7)
                    for n in "qkv":
                        dve.tensor_tensor(bias[n][32:33, :], b_stage[n][32:33, :], bias[n][32:33, :].bitcast(F32),
                                          ALU.subtract).then_inc(lo_made, 1)
                    dve.wait_ge(router_psum, 1)
                    dve.tensor_copy(router_t[:].rearrange("p c e -> p (c e)"), bank[7][:, 0:C * E]).then_inc(router_made, 1)

                    def lo_of(dst, src, hi, relu):
                        if relu:
                            return dve.scalar_tensor_tensor(dst, src, 0.0, hi.bitcast(F32), ALU.max, ALU.subtract)
                        return dve.tensor_tensor(dst, src, hi.bitcast(F32), ALU.subtract)

                    def norm_stats(n, src, g, first=False):
                        for t in range(T):
                            i = dve.bn_stats(st[n][:, t, :], src[:, t, :])
                        i.then_inc(stats_step[n], 1)
                        wait_apart(dve, stats_step[n], 2 * g + 1)
                        for t in range(T):
                            i = dve.bn_aggr(mv[n][:, t, :], st[n][:, t, :])
                        i.then_inc(stats_step[n], 1)
                        if not first:
                            dve.wait_ge(rstd_ready[n], g)
                        dve.wait_ge(stats_step[n], 2 * g + 2)
                        dve.tensor_scalar(neg_mean[n][:], mv[n][:, :, 0], -1.0, None, ALU.mult)
                        dve.tensor_scalar(var_eps[n][:], mv[n][:, :, 1], EPS, None, ALU.add).then_inc(var_ready[n], 1)

                    def stats1(g, first=False):
                        dve.wait_ge(xnorm_loaded, 16 * g + 16)
                        norm_stats("1", x_norm, g, first)

                    def stats2(g, first=False):
                        dve.wait_ge(x1_ready, 2 * g + 2)
                        norm_stats("2", x1, g, first)

                    def xnT(g):
                        for c in range(C):
                            dve.wait_ge(xnT_hi_ready, 2 * g + c + 1)
                            lo_of(xnT_lo[:, c, :], bank[2 + c][:], xnT_hi[:, c, :], False).then_inc(xnT_lo_ready, 1)

                    def qk(g, u):
                        dve.wait_ge(qk_hi_ready, 4 * g + u + 1)
                        lo_of(qk_lo[:, u, :], bank[4 + u][:], qk_hi[:, u, :], True).then_inc(qk_lo_ready, 1)

                    def wide(ap):
                        return ap.to_broadcast([P, T, E])

                    def route_choose(g):
                        step = [0]

                        def then(i):
                            step[0] += 1
                            i.then_inc(route_step, 1)
                            dve.wait_ge(route_step, ROUTE * g + step[0])

                        dve.wait_ge(logits_psum, g + 1)
                        step[0] += 1
                        dve.tensor_copy(logits[:].rearrange("p t e -> p (t e)"), bank[3][:, 0:T * E]).then_inc(route_step, 1)
                        wait_apart(dve, route_step, ROUTE * g + step[0])
                        for t in range(T):
                            i = dve.max(top8[:, t, :], logits[:, t, :])
                        then(i)
                        dve.tensor_tensor(shifted[:], logits[:], wide(top8[:, :, 0:1]), ALU.subtract).then_inc(expo_in, 1)
                        for t in range(T):
                            i = dve.max_index(top8_at[:, t, :], top8[:, t, :], logits[:, t, :])
                        then(i)
                        then(dve.tensor_copy(top2_at[:], top8_at[:, :, 0:2]))
                        for k in range(2):
                            i = dve.tensor_tensor(is_top[:, k], expert_no[:].unsqueeze(1).to_broadcast([P, T, E]),
                                                  wide(top2_at[:, :, k:k + 1]), ALU.is_equal)
                        then(i)
                        dve.tensor_tensor(chosen_bf[:], is_top[:, 0], is_top[:, 1], ALU.add).then_inc(chosen_ready, 1)
                        return step[0]

                    def route_weigh(g, done):
                        step = [done]

                        def then(i):
                            step[0] += 1
                            i.then_inc(route_step, 1)
                            dve.wait_ge(route_step, ROUTE * g + step[0])

                        then(dve.tensor_tensor(chosen[:], is_top[:, 0], is_top[:, 1], ALU.add))
                        dve.wait_ge(expo_ready, g + 1)
                        then(dve.tensor_reduce(gate_sum[:, 0, :], expo[:], AX.X, ALU.add))
                        then(dve.reciprocal(gate_sum[:, 1, :], gate_sum[:, 0, :]))
                        then(dve.tensor_tensor(gates[:, 0], expo[:], wide(gate_sum[:, 1, :].unsqueeze(2)), ALU.mult))
                        then(dve.tensor_tensor(gates[:, 1], gates[:, 0], chosen[:], ALU.mult))
                        then(dve.tensor_reduce(gate_sum[:, 2, :], gates[:, 1], AX.X, ALU.add))
                        then(dve.tensor_scalar(gate_sum[:, 3, :], gate_sum[:, 2, :], 1e-12, None, ALU.max))
                        then(dve.reciprocal(gate_sum[:, 2, :], gate_sum[:, 3, :]))
                        dve.tensor_tensor(rows[:, :, GATE:GATE + E], gates[:, 1], wide(gate_sum[:, 2, :].unsqueeze(2)),
                                          ALU.mult).then_inc(gates_ready, 1)
                        return step[0]

                    def route_place(g, done):
                        dve.wait_ge(rank_psum, g + 1)
                        ranks = bank[2][:, 0:T * E].rearrange("p (t e) -> p t e", t=T)
                        dve.tensor_tensor(place[:], ranks, carry[:].unsqueeze(1).to_broadcast([P, T, E]),
                                          ALU.add).then_inc(route_step, 1)
                        dve.wait_ge(route_step, ROUTE * g + done + 1)
                        dve.tensor_tensor(carry[:], carry[:], bank[2][:, T * E:(T + 1) * E], ALU.add)
                        for k in range(2):
                            i = dve.tensor_tensor(place_top[:, k], place[:], is_top[:, k], ALU.mult)
                        i.then_inc(route_step, 1)
                        dve.wait_ge(route_step, ROUTE * g + done + 2)
                        dve.tensor_reduce(slot_f[:], place_top[:], AX.X, ALU.add).then_inc(route_step, 1)
                        assert done + 3 == ROUTE
                        dve.wait_ge(route_step, ROUTE * g + ROUTE)
                        dve.tensor_copy(slot[:], slot_f[:]).then_inc(slots_ready, 1)

                    stats1(0, True)
                    xnT(0)
                    for u in range(2 * C):
                        qk(0, u)
                    stats1(1)

                    def graph(g, first=False, second=False, last=False, load_after=True):
                        if not first:
                            dve.wait_ge(probT_psum, 4 * g)
                        dve.wait_ge(adj_loaded, 16 * g + 16)

                        def times_mask(t):
                            dve.wait_ge(score_psum, 4 * g + t + 1)
                            dve.scalar_tensor_tensor(
                                prob[:, t, :].rearrange("q (t p) -> q t p", t=T),
                                bank[4 + t][:].rearrange("q (t p) -> q t p", t=T), -1.0,
                                adj_t[:, t, :].rearrange("q (p t) -> q t p", t=T), ALU.mult, ALU.mult).then_inc(masked, 1)

                        def add_mask(t):
                            wait_apart(dve, masked, 4 * g + t + 1)
                            dve.tensor_tensor_reduce(prob[:, t, :], prob[:, t, :], neg_mask[:, t, :], 1.0, BIG, ALU.add,
                                                     ALU.min, neg_max[:, t:t + 1]).then_inc(shift_ready, 1)

                        times_mask(0)
                        dve.wait_ge(negmask_ready, g + 1)
                        for t in range(1, T):
                            times_mask(t)
                            add_mask(t - 1)
                        add_mask(T - 1)
                        if not first:
                            stats2(g - 1, second)
                        for i in range(2):
                            dve.wait_ge(v_hi_ready, 2 * g + i + 1)
                            lo_of(v_lo[:, 2 * i:2 * i + 2, :].rearrange("p t d -> p (t d)"), bank[i][:],
                                  v_hi[:, 2 * i:2 * i + 2, :].rearrange("p t d -> p (t d)"), True).then_inc(v_lo_ready, 1)
                        for m in range(T):
                            dve.wait_ge(probT_hi_ready, 4 * g + m + 1)
                            lo_of(probT_lo[:, m, :], bank[4 + m][:], probT_hi[:, m, :], False).then_inc(probT_lo_ready, 1)
                        dve.reciprocal(row_inv[:], row_sum[:]).then_inc(inv_ready, 1)
                        if not last:
                            xnT(g + 1)
                        if load_after:
                            stats1(g + 2)
                        for c in range(C):
                            dve.wait_ge(o_hi_ready, 2 * g + c + 1)
                            lo_of(oT_lo[:, c, :], bank[c][:], oT_hi[:, c, :], False).then_inc(o_lo_ready, 1)
                        if not last:
                            for u in range(3):
                                qk(g + 1, u)
                        if not first:
                            done = route_choose(g - 1)
                        if not last:
                            qk(g + 1, 3)
                        if not first:
                            done = route_weigh(g - 1, done)
                            route_place(g - 1, done)
                        dve.wait_ge(inv_ready, g + 1)
                        if not first:
                            dve.wait_ge(base_stored, 16 * g)
                        dve.wait_ge(xres_loaded, 16 * g + 16)
                        for i in range(2):
                            dve.wait_ge(y_psum, 2 * g + i + 1)
                            for j in range(2):
                                t = 2 * i + j
                                dve.scalar_tensor_tensor(y_sb[:, t, :], bank[i][:, j * D:(j + 1) * D], row_inv[:, t:t + 1],
                                                         bo_rows[:], ALU.mult, ALU.add).then_inc(y_ready, 1)
                        for i in range(2):
                            dve.wait_ge(y_ready, 4 * g + 2 * i + 2)
                            dve.scalar_tensor_tensor(x1[:, 2 * i:2 * i + 2, :], y_sb[:, 2 * i:2 * i + 2, :], 0.0,
                                                     x_res[:, 2 * i:2 * i + 2, :], ALU.max, ALU.add).then_inc(x1_ready, 1)

                    graph(0, first=True)
                    graph(1, second=True)
                    with dve.Fori(2, G - 2) as g:
                        graph(g)
                    graph(G - 2, load_after=False)
                    graph(G - 1, last=True, load_after=False)
                    stats2(G - 1)
                    done = route_choose(G - 1)
                    done = route_weigh(G - 1, done)
                    route_place(G - 1, done)

                @block.tensor
                def _(pe):
                    pe.wait_ge(consts_made, 1)
                    pe.wait_ge(loaded, 16 * SETUP_LOADS)
                    for c in range(C):
                        i = pe.transpose(bank[7][:, c * E:(c + 1) * E], router_rows[:, c * P:(c + 1) * P], ident[0:E, 0:E])
                    i.then_inc(router_psum, 1)
                    pe.wait_ge(lo_made, 7)
                    pe.wait_ge(router_made, 1)

                    def split3(dst, a_hi, a_lo, b_hi, b_lo, start, stop):
                        pe.matmul(dst, a_hi, b_hi, start=start, stop=False)
                        pe.matmul(dst, a_hi, b_lo, start=False, stop=False)
                        return pe.matmul(dst, a_lo, b_hi, start=False, stop=stop)

                    def xnT(g):
                        pe.wait_ge(xn_ready, g + 1)
                        for c in range(C):
                            for t in range(T):
                                i = pe.transpose(bank[2 + c][:, t * P:(t + 1) * P], xn[:, t, c * P:(c + 1) * P], ident[:])
                            i.then_inc(xnT_psum, 1)

                    def qk(g, u):
                        n, h = "qk"[u // C], u % C
                        dst = bank[4 + u][:]
                        pe.matmul(dst, bias[n][:, h * P:(h + 1) * P], ones[:], start=True, stop=False)
                        for c in range(C):
                            i = split3(dst, w_hi[n][:, c, h * P:(h + 1) * P], w_lo[n][:, c, h * P:(h + 1) * P],
                                       xnT_hi[:, c, :], xnT_lo[:, c, :], False, c == C - 1)
                        i.then_inc(qk_psum, 1)

                    def route_in(g):
                        pe.wait_ge(xn2_ready, g + 1)
                        for c in range(C):
                            for t in range(T):
                                i = pe.transpose(bank[2 + c][:, t * P:(t + 1) * P], rows[:, t, c * P:(c + 1) * P], ident[:])
                            i.then_inc(xn2T_psum, 1)

                    def route_logitsT(g):
                        pe.wait_ge(xn2T_ready, 2 * g + 2)
                        for c in range(C):
                            i = pe.matmul(bank[2][0:E, :], router_t[:, c, :], xn2T[:, c, :], start=(c == 0), stop=(c == C - 1))
                        i.then_inc(logitsT_psum, 1)

                    def route_logits(g):
                        wait_apart(pe, logitsT_ready, g + 1)
                        for t in range(T):
                            i = pe.transpose(bank[3][:, t * E:(t + 1) * E], logitsT[:, t * P:(t + 1) * P], ident[0:E, 0:E])
                        i.then_inc(logits_psum, 1)

                    def route_ranks(g):
                        pe.wait_ge(chosen_ready, g + 1)
                        for t in range(T + 1):
                            dst = bank[2][:, t * E:(t + 1) * E]
                            if t < T:
                                i = pe.matmul(dst, before[:], chosen_bf[:, t, :], start=True, stop=(t == 0))
                            for s in range(t):
                                i = pe.matmul(dst, ones_bf[:], chosen_bf[:, s, :], start=(t == T and s == 0), stop=(s == t - 1))
                        i.then_inc(rank_psum, 1)

                    xnT(0)
                    pe.wait_ge(xnT_hi_ready, 2)
                    pe.wait_ge(xnT_lo_ready, 2)
                    for u in range(2 * C):
                        qk(0, u)

                    def graph(g, first=False, last=False):
                        pe.wait_ge(qk_hi_ready, 4 * g + 4)
                        pe.wait_ge(qk_lo_ready, 4 * g + 4)
                        for t in range(T):
                            for c in range(C):
                                i = split3(bank[4 + t][:], qk_hi[:, c, t * P:(t + 1) * P], qk_lo[:, c, t * P:(t + 1) * P],
                                           qk_hi[:, C + c, :], qk_lo[:, C + c, :], c == 0, c == C - 1)
                            i.then_inc(score_psum, 1)
                        for i2 in range(2):
                            if not first:
                                pe.wait_ge(y_ready, 4 * g - 2 + 2 * i2)
                            for j in range(2):
                                t = 2 * i2 + j
                                dst = bank[i2][:, j * D:(j + 1) * D]
                                pe.matmul(dst, ones[:, 0:P], bias["v"][:], start=True, stop=False)
                                for c in range(C):
                                    i = split3(dst, xnT_hi[:, c, t * P:(t + 1) * P], xnT_lo[:, c, t * P:(t + 1) * P],
                                               w_hi["v"][:, c, :], w_lo["v"][:, c, :], False, c == C - 1)
                            i.then_inc(v_psum, 1)
                        if not last:
                            xnT(g + 1)
                        pe.wait_ge(prob_ready, 4 * g + 4)
                        for m in range(T):
                            for t in range(T):
                                i = pe.transpose(bank[4 + m][:, t * P:(t + 1) * P], prob[:, t, m * P:(m + 1) * P], ident[:])
                            i.then_inc(probT_psum, 1)
                        pe.wait_ge(v_lo_ready, 2 * g + 2)
                        for m in range(T):
                            pe.wait_ge(probT_hi_ready, 4 * g + m + 1)
                            pe.wait_ge(probT_lo_ready, 4 * g + m + 1)
                            for c in range(C):
                                i = split3(bank[c][:], v_hi[:, m, c * P:(c + 1) * P], v_lo[:, m, c * P:(c + 1) * P],
                                           probT_hi[:, m, :], probT_lo[:, m, :], m == 0, m == T - 1)
                                if m == T - 1:
                                    i.then_inc(o_psum, 1)
                        if not last:
                            pe.wait_ge(xnT_hi_ready, 2 * g + 4)
                            pe.wait_ge(xnT_lo_ready, 2 * g + 4)
                        if not first:
                            route_in(g - 1)
                        if not last:
                            qk(g + 1, 0)
                        if not first:
                            route_logitsT(g - 1)
                        if not last:
                            qk(g + 1, 1)
                            qk(g + 1, 2)
                        if not first:
                            route_logits(g - 1)
                        if not last:
                            qk(g + 1, 3)
                        if not first:
                            route_ranks(g - 1)
                        pe.wait_ge(o_hi_ready, 2 * g + 2)
                        pe.wait_ge(o_lo_ready, 2 * g + 2)
                        for i2 in range(2):
                            for j in range(2):
                                t = 2 * i2 + j
                                dst = bank[i2][:, j * D:(j + 1) * D]
                                for c in range(C):
                                    i = split3(dst, oT_hi[:, c, t * P:(t + 1) * P], oT_lo[:, c, t * P:(t + 1) * P],
                                               w_hi["o"][:, c, :], w_lo["o"][:, c, :], c == 0, c == C - 1)
                            i.then_inc(y_psum, 1)

                    graph(0, first=True)
                    with pe.Fori(1, G - 1) as g:
                        graph(g)
                    graph(G - 1, last=True)
                    pe.wait_ge(slots_ready, G - 1)
                    route_in(G - 1)
                    route_logitsT(G - 1)
                    route_logits(G - 1)
                    route_ranks(G - 1)

        with ExitStack() as ph:
            MAT = C * D
            WCOLS = 4 * MAT + D
            experts = sb(ph, "experts", [P, E, WCOLS], F32R)
            b1_all = sb(ph, "b1_all", [P, E, C], F32)
            now1 = sb(ph, "now1", [P, 2, 2 * MAT], F32R)
            now2 = sb(ph, "now2", [P, 2, 2 * MAT + D], F32R)
            b1_now = sb(ph, "b1_now", [P, 2, C], F32)
            stage = sb(ph, "stage", [P, 4, MAT], F32)
            b2_stage = sb(ph, "b2_stage", [P, 2, D], F32)
            b1_rows = sb(ph, "b1_rows", [E, D], F32)
            pad = sb(ph, "pad", [P, T, ROW], F32)
            pad_id = sb(ph, "pad_id", [P, T], F32)

            table = sb(ph, "table", [P, 8, E], F32)
            table_i = sb(ph, "table_i", [P, 2, E], I32)
            block_no = sb(ph, "block_no", [P, NBLOCKS], F32)
            block_at = sb(ph, "block_at", [P, NBLOCKS], F32)
            block_e = sb(ph, "block_e", [P, 4, NBLOCKS], F32)
            ended = sb(ph, "ended", [P, NBLOCKS, E], F32)
            inside = sb(ph, "inside", [P, NBLOCKS, E], F32)
            start_of = sb(ph, "start_of", [P, NBLOCKS, E], F32)
            first_row = sb(ph, "first_row", [P, NBLOCKS], I32)
            expert_of = sb(ph, "expert_of", [P, NBLOCKS], I32)

            xrow = sb(ph, "xrow", [P, 2, T, ROW], F32)
            token = sb(ph, "token", [P, 2, T], U32)
            gate = sb(ph, "gate", [P, 2, T], F32)
            xT_hi = sb(ph, "xT_hi", [P, C, BLOCK], F32R)
            xT_lo = sb(ph, "xT_lo", [P, C, BLOCK], F32R)
            h_sb = sb(ph, "h_sb", [P, C, BLOCK], F32)
            h_hi = sb(ph, "h_hi", [P, 2, C, BLOCK], F32R)
            h_lo = sb(ph, "h_lo", [P, 2, C, BLOCK], F32R)
            y = sb(ph, "y", [P, 2, T, D], F32)

            expert_loaded = [sem(f"expert_loaded{i}") for i in range(4)]
            b2_loaded = [sem(f"b2_loaded{i}") for i in range(2)]
            b1_loaded = sem("b1_loaded")
            b2_zeroed = sem("b2_zeroed")
            b1_psum = sem("b1_psum")
            b1_made = sem("b1_made")
            experts_hi = sem("experts_hi")
            experts_lo = sem("experts_lo")
            pad_step = sem("pad_step")
            pad_made = sem("pad_made")
            table_step = sem("table_step")
            tables_made = sem("tables_made")
            xrow_loaded = [sem(f"xrow_loaded{q}") for q in range(2)]
            picked = sem("picked")
            now1_ready = sem("now1_ready")
            now2_ready = sem("now2_ready")
            xT_psum = sem("xT_psum")
            xT_hi_done = sem("xT_hi_done")
            xT_lo_done = sem("xT_lo_done")
            h_psum = sem("h_psum")
            h_ready = sem("h_ready")
            h_hi_done = sem("h_hi_done")
            h_lo_done = sem("h_lo_done")
            ye_psum = sem("ye_psum")
            ye_ready = sem("ye_ready")
            added = sem("added")

            with nc.Block() as block:

                @block.sync
                def _(sp):
                    for e in range(E):
                        for m, w in enumerate((w1, w2)):
                            s = (2 * e + m) % 4
                            if e >= 2:
                                sp.wait_ge(experts_lo, 3 * (e - 2) + m + 1)
                            sp.dma_start(stage[:, s, :].rearrange("p (c n) -> p c n", c=C),
                                         w[e].rearrange("(c p) n -> p c n", p=P)).then_inc(expert_loaded[s], 16)
                        sp.wait_ge(b2_zeroed, 1)
                        if e >= 2:
                            sp.wait_ge(experts_lo, 3 * (e - 2) + 3)
                        for row in (0, 32):
                            sp.dma_start(b2_stage[row:row + 1, e % 2, :], b2[e:e + 1, :]).then_inc(b2_loaded[e % 2], 16)
                        if e == 0:
                            sp.dma_start(b1_rows[:], b1).then_inc(b1_loaded, 16)
                    sp.wait_ge(pad_made, 1)
                    sp.wait_ge(tables_made, 1)
                    sp.dma_start(out_v[G * P:(G + 1) * P, :].rearrange("p (t d) -> p t d", t=T),
                                 pad[:, :, 0:D]).then_inc(pad_stored, 16)
                    sp.dma_start(rows_dram[DUMMY:DUMMY + BLOCK, :].rearrange("(p t) r -> p (t r)", t=T),
                                 pad[:].rearrange("p t r -> p (t r)")).then_inc(pad_stored, 16)
                    for e in range(E):
                        at = sp.value_load(table_i[0:1, 1, e:e + 1], min_val=0, max_val=DUMMY - BLOCK)
                        sp.dma_start(rows_dram[bass.ds(at, BLOCK), :].rearrange("(p t) r -> p (t r)", t=T),
                                     pad[:].rearrange("p t r -> p (t r)")).then_inc(pad_stored, 16)
                    sp.wait_ge(pad_stored, 16 * (E + 2))

                    def load_rows(j, q, first=False):
                        at = sp.value_load(first_row[0:1, bass.ds(j, 1)], min_val=0, max_val=DUMMY)
                        if not first:
                            wait_apart(sp, xT_psum, 2 * j - 2)
                            wait_apart(sp, picked, j - 1)
                        sp.dma_start(xrow[:, q].rearrange("p t r -> p (t r)"),
                                     rows_dram[bass.ds(at, BLOCK), :].rearrange("(p t) r -> p (t r)", t=T)).then_inc(xrow_loaded[q], 16)

                    load_rows(0, 0, True)
                    load_rows(1, 1, True)
                    with sp.Fori(1, (NBLOCKS - 1) // 2) as i:
                        load_rows(2 * i, 0)
                        load_rows(2 * i + 1, 1)
                    load_rows(NBLOCKS - 1, 0)

                @block.gpsimd
                def _(pool):
                    for s in range(2):
                        z = pool.memset(b2_stage[:, s, :], 0.0)
                    z.then_inc(b2_zeroed, 1)
                    pool.memset(pad[:], 0.0).then_inc(pad_step, 1)
                    pool.iota(pad_id[:], [[1, T]], TOKENS, T, allow_small_or_imprecise_dtypes=True).then_inc(pad_step, 1)
                    pool.iota(block_no[:], [[1, NBLOCKS]], 0, 0, allow_small_or_imprecise_dtypes=True).then_inc(pad_step, 1)
                    pool.wait_ge(pad_step, 3)
                    pool.tensor_copy(pad[:, :, ID].bitcast(U32), pad_id[:]).then_inc(pad_made, 1)

                    def add_rows(j, q, first=False):
                        if not first:
                            wait_apart(pool, added, 16 * T * j)
                        wait_apart(pool, picked, j + 1)
                        wait_apart(pool, ye_ready, 2 * j + 2)
                        for t in range(T):
                            pool.indirect_dma_start(out, bass.IndirectOffsetOnAxis(ap=token[:, q, t:t + 1], axis=0),
                                                    y[:, q, t, :], None, compute_op=ALU.add).then_inc(added, 16)

                    add_rows(0, 0, True)
                    add_rows(1, 1)
                    with pool.Fori(1, (NBLOCKS - 1) // 2) as i:
                        add_rows(2 * i, 0)
                        add_rows(2 * i + 1, 1)
                    add_rows(NBLOCKS - 1, 0)
                    pool.wait_ge(added, 16 * T * NBLOCKS)

                @block.scalar
                def _(act):
                    for e in range(E):
                        for m in range(2):
                            s = (2 * e + m) % 4
                            act.wait_ge(expert_loaded[s], 16 * (e // 2 + 1))
                            act.copy(experts[:, e, 2 * m * MAT:(2 * m + 1) * MAT], stage[:, s, :]).then_inc(experts_hi, 1)
                        act.wait_ge(b2_loaded[e % 2], 32 * (e // 2 + 1))
                        act.copy(experts[:, e, 4 * MAT:], b2_stage[:, e % 2, :]).then_inc(experts_hi, 1)

                    def x_hi(j):
                        for c in range(C):
                            act.wait_ge(xT_psum, 2 * j + c + 1)
                            act.copy(xT_hi[:, c, :], bank[c][:]).then_inc(xT_hi_done, 1)

                    def hidden(j, q, first=False):
                        act.wait_ge(now1_ready, j + 1)
                        if not first:
                            act.wait_ge(h_lo_done, 2 * j)
                        for c in range(C):
                            act.wait_ge(h_psum, 2 * j + c + 1)
                            act.activation(h_sb[:, c, :], bank[2 + c][:], ACT.Gelu, bias=b1_now[:, q, c:c + 1]).then_inc(h_ready, 1)

                    def weigh(j, q, first=False):
                        act.wait_ge(picked, j + 1)
                        if not first:
                            act.wait_ge(added, 16 * T * (j - 1))
                        for i in range(2):
                            act.wait_ge(ye_psum, 2 * j + i + 1)
                            for t in (2 * i, 2 * i + 1):
                                k = act.activation(y[:, q, t, :], bank[4 + 2 * q + i][:, (t % 2) * D:(t % 2 + 1) * D], ACT.Copy,
                                                   scale=gate[:, q, t:t + 1])
                            k.then_inc(ye_ready, 1)

                    x_hi(0)
                    hidden(0, 0, True)
                    x_hi(1)
                    hidden(1, 1)
                    x_hi(2)
                    weigh(0, 0, True)
                    hidden(2, 0)
                    x_hi(3)
                    weigh(1, 1, True)
                    with act.Fori(1, (NBLOCKS - 3) // 2) as i:
                        for q in range(2):
                            hidden(2 * i + 1 + q, 1 - q)
                            x_hi(2 * i + 2 + q)
                            weigh(2 * i + q, q)
                    hidden(NBLOCKS - 2, 1)
                    x_hi(NBLOCKS - 1)
                    weigh(NBLOCKS - 3, 0)
                    hidden(NBLOCKS - 1, 0)
                    weigh(NBLOCKS - 2, 1)
                    weigh(NBLOCKS - 1, 0)

                @block.vector
                def _(dve):
                    step = [0]

                    def then(i):
                        step[0] += 1
                        i.then_inc(table_step, 1)
                        dve.wait_ge(table_step, step[0])

                    def over_blocks(ap):
                        return ap.unsqueeze(1).to_broadcast([P, NBLOCKS, E])

                    def over_experts(ap):
                        return ap.unsqueeze(2).to_broadcast([P, NBLOCKS, E])

                    REGION0, COUNT, BLOCKS, END, START = range(5)
                    dve.wait_ge(pad_made, 1)
                    then(dve.tensor_scalar(table[:, REGION0, :], expert_no[:], float(REGION), None, ALU.mult))
                    then(dve.tensor_tensor(table[:, COUNT, :], carry[:], table[:, REGION0, :], ALU.subtract))
                    then(dve.tensor_scalar(table_i[:, 0, :], table[:, COUNT, :], float(BLOCK - 1), None, ALU.add))
                    then(dve.tensor_scalar(table_i[:, 1, :], table_i[:, 0, :], 9, None, ALU.logical_shift_right))
                    then(dve.tensor_copy(table[:, BLOCKS, :], table_i[:, 1, :]))
                    then(dve.tensor_copy(table[:, END, :], table[:, BLOCKS, :]))
                    for e in range(1, E):
                        then(dve.tensor_tensor(table[:, END, e:e + 1], table[:, END, e - 1:e], table[:, BLOCKS, e:e + 1], ALU.add))
                    then(dve.tensor_tensor(table[:, START, :], table[:, END, :], table[:, BLOCKS, :], ALU.subtract))
                    then(dve.scalar_tensor_tensor(table[:, START, :], table[:, START, :], -float(BLOCK), table[:, REGION0, :],
                                                  ALU.mult, ALU.add))
                    then(dve.tensor_copy(table_i[:, 1, :], carry[:]))
                    then(dve.tensor_tensor(ended[:], over_experts(block_no[:]), over_blocks(table[:, END, :]), ALU.is_ge))
                    dve.tensor_scalar(inside[:, :, 0:1], ended[:, :, 0:1], -1.0, 1.0, ALU.mult, ALU.add)
                    then(dve.tensor_tensor(inside[:, :, 1:E], ended[:, :, 0:E - 1], ended[:, :, 1:E], ALU.subtract))
                    then(dve.tensor_scalar(block_at[:], block_no[:], float(BLOCK), float(-DUMMY), ALU.mult, ALU.add))
                    then(dve.tensor_tensor(start_of[:], over_experts(block_at[:]), over_blocks(table[:, START, :]), ALU.add))
                    then(dve.tensor_tensor(start_of[:], start_of[:], inside[:], ALU.mult))
                    then(dve.tensor_reduce(block_e[:, 0, :], start_of[:], AX.X, ALU.add))
                    then(dve.tensor_scalar(first_row[:], block_e[:, 0, :], float(DUMMY), None, ALU.add))
                    then(dve.tensor_reduce(block_e[:, 1, :], ended[:], AX.X, ALU.add))
                    then(dve.tensor_scalar(expert_of[:], block_e[:, 1, :], float(E - 1), None, ALU.min))
                    dve.sem_inc(tables_made, 1)

                    for e in range(E):
                        for m in range(2):
                            dve.wait_ge(experts_hi, 3 * e + m + 1)
                            dve.tensor_tensor(experts[:, e, (2 * m + 1) * MAT:(2 * m + 2) * MAT], stage[:, (2 * e + m) % 4, :],
                                              experts[:, e, 2 * m * MAT:(2 * m + 1) * MAT].bitcast(F32),
                                              ALU.subtract).then_inc(experts_lo, 1)
                        dve.wait_ge(experts_hi, 3 * e + 3)
                        dve.tensor_tensor(experts[32:33, e, 4 * MAT:], b2_stage[32:33, e % 2, :],
                                          experts[32:33, e, 4 * MAT:].bitcast(F32), ALU.subtract).then_inc(experts_lo, 1)
                    dve.wait_ge(b1_psum, 1)
                    dve.tensor_copy(b1_all[:], bank[7][:, 0:C * E].rearrange("p (c e) -> p e c", c=C)).then_inc(b1_made, 1)
                    dve.wait_ge(b1_made, 1)
                    dve.wait_ge(experts_lo, 3 * E)

                    def take1(j, q, first=False):
                        e = dve.value_load(expert_of[0:1, bass.ds(j, 1)], min_val=0, max_val=E - 1)
                        if not first:
                            dve.wait_ge(h_ready, 2 * j - 2)
                        dve.tensor_copy(b1_now[:, q], b1_all[:, bass.ds(e, 1), :].rearrange("p o c -> p (o c)"))
                        dve.tensor_copy(now1[:, q], experts[:, bass.ds(e, 1), 0:2 * MAT].rearrange("p o c -> p (o c)")).then_inc(now1_ready, 1)

                    def take2(j, q, first=False):
                        e = dve.value_load(expert_of[0:1, bass.ds(j, 1)], min_val=0, max_val=E - 1)
                        if not first:
                            dve.wait_ge(ye_psum, 2 * j - 2)
                        dve.tensor_copy(now2[:, q], experts[:, bass.ds(e, 1), 2 * MAT:].rearrange("p o c -> p (o c)")).then_inc(now2_ready, 1)

                    def pick(j, q, pair, first=False):
                        e = dve.value_load(expert_of[0:1, bass.ds(j, 1)], min_val=0, max_val=E - 1)
                        dve.wait_ge(xrow_loaded[q], 16 * pair + 16)
                        if not first:
                            dve.wait_ge(added, 16 * T * (j - 1))
                            dve.wait_ge(ye_ready, 2 * j - 2)
                        dve.tensor_copy(token[:, q], xrow[:, q, :, ID].bitcast(U32))
                        dve.tensor_copy(gate[:, q], xrow[:, q, :, bass.ds(e + GATE, 1)].rearrange("p t o -> p (t o)")).then_inc(picked, 1)

                    def x_lo(j):
                        for c in range(C):
                            dve.wait_ge(xT_hi_done, 2 * j + c + 1)
                            dve.tensor_tensor(xT_lo[:, c, :], bank[c][:], xT_hi[:, c, :].bitcast(F32),
                                              ALU.subtract).then_inc(xT_lo_done, 1)

                    def hidden_hi(j, q, first=False):
                        if not first:
                            dve.wait_ge(ye_psum, 2 * j - 2)
                        for c in range(C):
                            dve.wait_ge(h_ready, 2 * j + c + 1)
                            dve.tensor_copy(h_hi[:, q, c, :], h_sb[:, c, :]).then_inc(h_hi_done, 1)

                    def hidden_lo(j, q):
                        for c in range(C):
                            dve.wait_ge(h_hi_done, 2 * j + c + 1)
                            dve.tensor_tensor(h_lo[:, q, c, :], h_sb[:, c, :], h_hi[:, q, c, :].bitcast(F32),
                                              ALU.subtract).then_inc(h_lo_done, 1)

                    def around(j, q, pair, first=False, last=False):
                        if not last:
                            take1(j + 1, q, first)
                        hidden_hi(j, 1 - q, isinstance(j, int) and j < 2)
                        if not last:
                            x_lo(j + 1)
                        hidden_lo(j, 1 - q)
                        take2(j, 1 - q, isinstance(j, int) and j < 2)
                        if not last:
                            pick(j + 1, q, pair, first)

                    take1(0, 0, True)
                    pick(0, 0, 0, True)
                    x_lo(0)
                    around(0, 1, 0, first=True)
                    around(1, 0, 1)
                    with dve.Fori(1, (NBLOCKS - 1) // 2) as i:
                        for q in range(2):
                            around(2 * i + q, 1 - q, i + q)
                    around(NBLOCKS - 1, 1, 0, last=True)

                @block.tensor
                def _(pe):
                    pe.wait_ge(b1_loaded, 16)
                    for c in range(C):
                        i = pe.transpose(bank[7][:, c * E:(c + 1) * E], b1_rows[:, c * P:(c + 1) * P], ident[0:E, 0:E])
                    i.then_inc(b1_psum, 1)

                    def split3(dst, a_hi, a_lo, b_hi, b_lo, start, stop):
                        pe.matmul(dst, a_hi, b_hi, start=start, stop=False)
                        pe.matmul(dst, a_hi, b_lo, start=False, stop=False)
                        return pe.matmul(dst, a_lo, b_hi, start=False, stop=stop)

                    def mat(now, q, half, c):
                        return now[:, q, half * MAT + c * D:half * MAT + (c + 1) * D]

                    def turn(j, q, pair, first=False):
                        pe.wait_ge(xrow_loaded[q], 16 * pair + 16)
                        if not first:
                            pe.wait_ge(xT_lo_done, 2 * j)
                        for c in range(C):
                            for t in range(T):
                                i = pe.transpose(bank[c][:, t * P:(t + 1) * P], xrow[:, q, t, c * P:(c + 1) * P], ident[:])
                            i.then_inc(xT_psum, 1)

                    def layer1(j, q, first=False):
                        pe.wait_ge(now1_ready, j + 1)
                        pe.wait_ge(xT_hi_done, 2 * j + 2)
                        pe.wait_ge(xT_lo_done, 2 * j + 2)
                        if not first:
                            pe.wait_ge(h_ready, 2 * j)
                        for h in range(C):
                            for c in range(C):
                                i = split3(bank[2 + h][:], mat(now1, q, 0, c)[:, h * P:(h + 1) * P], mat(now1, q, 1, c)[:, h * P:(h + 1) * P],
                                           xT_hi[:, c, :], xT_lo[:, c, :], c == 0, c == C - 1)
                            i.then_inc(h_psum, 1)

                    def layer2(j, q, first=False):
                        pe.wait_ge(now2_ready, j + 1)
                        pe.wait_ge(h_hi_done, 2 * j + 2)
                        pe.wait_ge(h_lo_done, 2 * j + 2)
                        if not first:
                            pe.wait_ge(ye_ready, 2 * j - 2)
                        for i2 in range(2):
                            for t in (2 * i2, 2 * i2 + 1):
                                dst = bank[4 + 2 * q + i2][:, (t % 2) * D:(t % 2 + 1) * D]
                                pe.matmul(dst, ones[:, 0:P], now2[:, q, 2 * MAT:], start=True, stop=False)
                                for c in range(C):
                                    i = split3(dst, h_hi[:, q, c, t * P:(t + 1) * P], h_lo[:, q, c, t * P:(t + 1) * P],
                                               mat(now2, q, 0, c), mat(now2, q, 1, c), False, c == C - 1)
                            i.then_inc(ye_psum, 1)

                    turn(0, 0, 0, True)
                    layer1(0, 0, True)
                    turn(1, 1, 0)
                    layer1(1, 1)
                    turn(2, 0, 1)
                    layer2(0, 0, True)
                    layer1(2, 0)
                    turn(3, 1, 1)
                    layer2(1, 1, True)
                    with pe.Fori(1, (NBLOCKS - 3) // 2) as i:
                        for q in range(2):
                            layer1(2 * i + 1 + q, 1 - q)
                            turn(2 * i + 2 + q, q, i + 1)
                            layer2(2 * i + q, q)
                    layer1(NBLOCKS - 2, 1)
                    turn(NBLOCKS - 1, 0, (NBLOCKS - 1) // 2)
                    layer2(NBLOCKS - 3, 0)
                    layer1(NBLOCKS - 1, 0)
                    layer2(NBLOCKS - 2, 1)
                    layer2(NBLOCKS - 1, 0)


_INS = ["x", "adj", "L0_gnn_Wv", "L0_gnn_bv", "L0_gnn_Wk", "L0_gnn_bk", "L0_gnn_Wq", "L0_gnn_bq", "L0_gnn_Wo",
        "L0_gnn_bo", "L0_ffn_router_w", "L0_ffn_w1", "L0_ffn_b1", "L0_ffn_w2", "L0_ffn_b2"]


def kernel(**inputs):
    import numpy as np
    import concourse.bacc as bacc
    from concourse.bass_utils import run_bass_kernel_spmd

    nc = bacc.Bacc("TRN2", target_bir_lowering=False, num_devices=1)
    arrays, args = {}, []
    for name in _INS:
        a = np.ascontiguousarray(inputs[name])
        arrays[f"in_{name}"] = a
        args.append(nc.dram_tensor(f"in_{name}", a.shape, mybir.dt.from_np(a.dtype), kind="ExternalInput").ap())
    g, n, d = inputs["x"].shape
    args.append(nc.dram_tensor("out_rows", [g * n + 512, d], F32, kind="ExternalOutput").ap())
    build_program(nc, *args)
    r = run_bass_kernel_spmd(nc, [arrays], core_ids=[0])
    return r.results[0]["out_rows"][:g * n].reshape(g, n, d)
```

```python
from contextlib import ExitStack

import concourse.bass as bass
from concourse import mybir

P = 128
F32 = mybir.dt.float32
F32R = mybir.dt.float32r
BF16 = mybir.dt.bfloat16
U32 = mybir.dt.uint32
I32 = mybir.dt.int32
ALU = mybir.AluOpType
ACT = mybir.ActivationFunctionType
AX = mybir.AxisListType

NEG = 9000000000000000.0
EPS = 1e-5
BIG = 3.0e38


def build_program(nc, x, adj, wv, bv, wk, bk, wq, bq, wo, bo, router_w, w1, b1, w2, b2, out):
    G, N, D = x.shape
    E = router_w.shape[0]
    T = N // P
    C = D // P
    TOKENS = G * N
    BLOCK = 512
    REGION = BLOCK + TOKENS
    DUMMY = E * REGION
    NBLOCKS = (2 * TOKENS + E * (BLOCK - 1)) // BLOCK
    ID = D
    GATE = D + 1
    ROW = 272
    assert G % 2 == 0 and GATE + E <= ROW and N == BLOCK == 4 * P and D == 2 * P

    rows_dram = nc.dram_tensor("rows_dram", [DUMMY + BLOCK, ROW], F32, kind="Internal").ap()

    x_rows = x.rearrange("g n d -> (g n) d")
    adj_rows = adj.rearrange("g n m -> (g n) m")

    def tiles(rows, g):
        at = bass.ds(g * N, N) if not isinstance(g, int) else slice(g * N, (g + 1) * N)
        return rows[at, :].rearrange("(t p) d -> p t d", p=P)

    with ExitStack() as whole:
        def sb(stack, name, shape, dt):
            return stack.enter_context(nc.sbuf_tensor(name, shape, dt))

        def sem(name):
            return whole.enter_context(nc.semaphore(name))

        bank = [whole.enter_context(nc.psum_tensor(f"bank{i}", [P, 512], F32)) for i in range(8)]

        loaded = sem("loaded")

        ident = sb(whole, "ident", [P, P], F32)
        ones = sb(whole, "ones", [P, P], F32R)
        before = sb(whole, "before", [P, P], BF16)
        ones_bf = sb(whole, "ones_bf", [P, P], BF16)
        expert_no = sb(whole, "expert_no", [P, E], F32)
        carry = sb(whole, "carry", [P, E], F32)

        MAT = C * D
        w12_lo = sb(whole, "w12_lo", [P, E, 2, MAT], F32R)
        w12_hi = sb(whole, "w12_hi", [P, E, 2, MAT], F32R)
        b2_all = sb(whole, "b2_all", [P, E, D], F32)
        b1_all = sb(whole, "b1_all", [P, E, C], F32)
        first_row = sb(whole, "first_row", [P, NBLOCKS], I32)
        expert_of = sb(whole, "expert_of", [P, NBLOCKS], I32)
        added_before = sb(whole, "added_before", [P, NBLOCKS], I32)
        experts_loaded = sem("experts_loaded")

        waited_apart = sem("waited_apart")
        consts_made = sem("consts_made")

        def early(g, n=2):
            return isinstance(g, int) and g < n

        def wait_apart(eng, what, value):
            eng.wait_ge(what, value)
            eng.sem_inc(waited_apart, 1)

        with ExitStack() as ph:
            w_hi = {n: sb(ph, f"w{n}_hi", [P, C, D], F32R) for n in "qkvo"}
            w_lo = {n: sb(ph, f"w{n}_lo", [P, C, D], F32R) for n in "qkvo"}
            bias_v = sb(ph, "bias_v", [P, D], F32R)
            bias_qk = sb(ph, "bias_qk", [P, 2, C], F32)
            bo_rows = sb(ph, "bo_rows", [P, D], F32)
            router_rows = sb(ph, "router_rows", [E, D], F32)
            router_t = sb(ph, "router_t", [P, C, E], F32)
            minus_half = sb(ph, "minus_half", [P, T], F32)
            id_f = sb(ph, "id_f", [P, T], F32)

            x_norm = sb(ph, "x_norm", [P, T, D], F32)
            x_res = sb(ph, "x_res", [P, T, D], F32)
            adj_t = sb(ph, "adj_t", [P, T, N], F32)
            neg_mask = sb(ph, "neg_mask", [P, T, N], F32)
            xn = sb(ph, "xn", [P, T, D], F32)
            xnT_hi = sb(ph, "xnT_hi", [P, C, N], F32R)
            xnT_lo = sb(ph, "xnT_lo", [P, C, N], F32R)
            room = w12_hi[:].rearrange("p e m n -> p (e m) n")
            assert MAT == N and 2 * E == 2 * (2 * C + T) and 2 * C == T
            qk_hi, qk_lo, probT_hi, probT_lo = (room[:, T * i:T * (i + 1), :] for i in range(4))
            v_hi = sb(ph, "v_hi", [P, T, D], F32R)
            v_lo = sb(ph, "v_lo", [P, T, D], F32R)
            prob = sb(ph, "prob", [P, T, N], F32)
            qk_f = prob
            oT_hi = sb(ph, "oT_hi", [P, C, N], F32R)
            oT_lo = sb(ph, "oT_lo", [P, C, N], F32R)
            y_sb = sb(ph, "y_sb", [P, T, D], F32)
            x1 = sb(ph, "x1", [P, T, D], F32)
            rows = sb(ph, "rows", [P, 2, T, ROW], F32)
            xn2T = sb(ph, "xn2T", [P, C, N], F32)

            neg_max = sb(ph, "neg_max", [P, T], F32)
            row_sum = sb(ph, "row_sum", [P, T], F32)
            row_inv = sb(ph, "row_inv", [P, T], F32)
            st = {n: sb(ph, f"st{n}", [P, T, 6], F32) for n in "12"}
            mv = {n: sb(ph, f"mv{n}", [P, T, 2], F32) for n in "12"}
            var_eps = {n: sb(ph, f"var_eps{n}", [P, T], F32) for n in "12"}
            neg_mean = {n: sb(ph, f"neg_mean{n}", [P, T], F32) for n in "12"}
            rstd = {n: sb(ph, f"rstd{n}", [P, T], F32) for n in "12"}
            norm_bias = {n: sb(ph, f"norm_bias{n}", [P, T], F32) for n in "12"}

            logitsT = sb(ph, "logitsT", [E, N], F32)
            logits = sb(ph, "logits", [P, T, E], F32)
            top8 = sb(ph, "top8", [P, T, 8], F32)
            top8_at = sb(ph, "top8_at", [P, T, 8], U32)
            top2_at = sb(ph, "top2_at", [P, T, 2], F32)
            is_top = sb(ph, "is_top", [P, 2, T, E], F32)
            chosen_bf = sb(ph, "chosen_bf", [P, T, E], BF16)
            shifted = sb(ph, "shifted", [P, T, E], F32)
            expo = sb(ph, "expo", [P, T, E], F32)
            gate_sum = sb(ph, "gate_sum", [P, 4, T], F32)
            gates = sb(ph, "gates", [P, T, E], F32)
            place = sb(ph, "place", [P, T, E], F32)
            place_top = sb(ph, "place_top", [P, 2, T, E], F32)
            slot_f = sb(ph, "slot_f", [P, 2, T], F32)
            slot = sb(ph, "slot", [P, 2, 2, T], U32)

            pad_id = sb(ph, "pad_id", [P, T], F32)
            table = sb(ph, "table", [P, 8, E], F32)
            table_i = sb(ph, "table_i", [P, 3, E], I32)
            block_no = sb(ph, "block_no", [P, NBLOCKS], F32)
            block_at = sb(ph, "block_at", [P, NBLOCKS], F32)
            block_e = sb(ph, "block_e", [P, 3, NBLOCKS], F32)
            odd_blocks = sb(ph, "odd_blocks", [P, NBLOCKS + NBLOCKS % 2], F32)

            xnorm_loaded = sem("xnorm_loaded")
            xres_loaded = sem("xres_loaded")
            adj_loaded = sem("adj_loaded")
            var_ready = {n: sem(f"var{n}_ready") for n in "12"}
            rstd_ready = {n: sem(f"rstd{n}_ready") for n in "12"}
            root_step = {n: sem(f"root{n}_step") for n in "12"}
            stats_step = {n: sem(f"stats{n}_step") for n in "12"}
            xn_ready = sem("xn_ready")
            xnT_psum = sem("xnT_psum")
            xnT_hi_ready = sem("xnT_hi_ready")
            xnT_lo_ready = sem("xnT_lo_ready")
            qk_psum = sem("qk_psum")
            qk_ready = sem("qk_ready")
            qk_hi_ready = sem("qk_hi_ready")
            qk_lo_ready = sem("qk_lo_ready")
            v_psum = sem("v_psum")
            v_hi_ready = sem("v_hi_ready")
            v_lo_ready = sem("v_lo_ready")
            score_psum = sem("score_psum")
            negmask_ready = sem("negmask_ready")
            masked = sem("masked")
            shift_ready = sem("shift_ready")
            prob_ready = sem("prob_ready")
            probT_psum = sem("probT_psum")
            probT_hi_ready = sem("probT_hi_ready")
            probT_lo_ready = sem("probT_lo_ready")
            o_psum = sem("o_psum")
            o_hi_ready = sem("o_hi_ready")
            o_lo_ready = sem("o_lo_ready")
            inv_ready = sem("inv_ready")
            y_psum = sem("y_psum")
            y_ready = sem("y_ready")
            x1_ready = sem("x1_ready")
            xn2_ready = sem("xn2_ready")
            base_ready = sem("base_ready")
            base_stored = sem("base_stored")
            xn2T_psum = sem("xn2T_psum")
            xn2T_ready = sem("xn2T_ready")
            logitsT_psum = sem("logitsT_psum")
            logitsT_ready = sem("logitsT_ready")
            logits_psum = sem("logits_psum")
            expo_in = sem("expo_in")
            expo_ready = sem("expo_ready")
            chosen_ready = sem("chosen_ready")
            rank_psum = sem("rank_psum")
            gates_ready = sem("gates_ready")
            ranks_read = sem("ranks_read")
            slots_ready = sem("slots_ready")
            id_ready = sem("id_ready")
            id_step = sem("id_step")
            scattered = [sem(f"scattered{q}") for q in range(2)]

            def rows_of(q, pair):
                return 16 * 2 * T * pair + (16 * (E + 2) if q == 1 else 0)

            route_step = sem("route_step")
            CHOOSE = 5
            ROUTE = CHOOSE + 7
            w_loaded = {n: sem(f"w{n}_loaded") for n in "qkvo"}
            ident_made = sem("ident_made")
            hi_made = sem("hi_made")
            lo_made = sem("lo_made")
            bias_zeroed = sem("bias_zeroed")
            router_psum = sem("router_psum")
            router_made = sem("router_made")
            pool_step = sem("pool_step")
            rows_zeroed = sem("rows_zeroed")
            experts_hi = sem("experts_hi")
            pad_made = sem("pad_made")
            table_step = sem("table_step")

            with nc.Block() as block:
                w_stage = {"q": prob[:, 0, :], "k": prob[:, 1, :], "v": prob[:, 2, :], "o": prob[:, 3, :]}
                bv_stage = y_sb[:, 2, :]
                b_rows = y_sb[0:E + 2, 3, :]
                w_in = {"q": wq, "k": wk, "v": wv, "o": wo}
                SMALL_LOADS = 2 + 2 + 3

                pad = rows[:, 1]
                spare = adj_t[:].rearrange("p t m -> p (t m)")
                ended, inside, start_of = (spare[:, i * NBLOCKS * E:(i + 1) * NBLOCKS * E].rearrange("p (b e) -> p b e", e=E)
                                           for i in range(3))
                assert 3 * NBLOCKS * E <= T * N

                @block.sync
                def _(sp):
                    sp.dma_start(x_norm[:], tiles(x_rows, 0)).then_inc(xnorm_loaded, 16)
                    for n in "qkvo":
                        sp.dma_start(w_stage[n].rearrange("p (c n) -> p c n", c=C),
                                     w_in[n].rearrange("(c p) n -> p c n", p=P)).then_inc(w_loaded[n], 16)
                    sp.dma_start(adj_t[:], tiles(adj_rows, 0)).then_inc(adj_loaded, 16)
                    sp.dma_start(x_res[:], tiles(x_rows, 0)).then_inc(xres_loaded, 16)
                    sp.wait_ge(xn_ready, 1)
                    sp.dma_start(x_norm[:], tiles(x_rows, 1)).then_inc(xnorm_loaded, 16)
                    for e in range(E):
                        for m, w in enumerate((w1, w2)):
                            sp.dma_start(w12_lo[:, e, m, :].bitcast(F32).rearrange("p (c n) -> p c n", c=C),
                                         w[e].rearrange("(c p) n -> p c n", p=P)).then_inc(experts_loaded, 16)
                    sp.dma_start(b2_all[:].rearrange("p e d -> p (e d)"),
                                 b2.rearrange("e d -> (e d)").partition_broadcast(P)).then_inc(experts_loaded, 16)

                    def graph(g, first=False, load_next=True, load_after=True):
                        if load_after:
                            wait_apart(sp, xn_ready, g + 2)
                            sp.dma_start(x_norm[:], tiles(x_rows, g + 2)).then_inc(xnorm_loaded, 16)
                        if load_next:
                            wait_apart(sp, masked, 4 * g + 4)
                            wait_apart(sp, negmask_ready, g + 1)
                            sp.dma_start(adj_t[:], tiles(adj_rows, g + 1)).then_inc(adj_loaded, 16)
                        if not first:
                            wait_apart(sp, x1_ready, 2 * g)
                            sp.dma_start(x_res[:], tiles(x_rows, g)).then_inc(xres_loaded, 16)
                            wait_apart(sp, base_ready, g)
                            sp.dma_start(tiles(out, g - 1), x1[:]).then_inc(base_stored, 16)

                    graph(0, first=True)
                    with sp.Fori(1, G - 2) as g:
                        graph(g)
                    graph(G - 2, load_after=False)
                    graph(G - 1, load_next=False, load_after=False)
                    sp.wait_ge(base_ready, G)
                    sp.dma_start(tiles(out, G - 1), x1[:]).then_inc(base_stored, 16)
                    sp.wait_ge(base_stored, 16 * G)

                @block.gpsimd
                def _(pool):
                    pool.memset(ident[:], 0.0).then_inc(pool_step, 1)
                    pool.memset(before[:], 1.0).then_inc(pool_step, 1)
                    pool.memset(minus_half[:], -0.5).then_inc(pool_step, 1)
                    pool.wait_ge(pool_step, 3)
                    pool.affine_select(out=ident[:], in_=ident[:], compare_op=ALU.not_equal, fill=1.0, base=0,
                                       pattern=[[-1, P]], channel_multiplier=1).then_inc(ident_made, 1)
                    pool.affine_select(out=before[:], in_=before[:], compare_op=ALU.is_gt, fill=0.0, base=0,
                                       pattern=[[1, P]], channel_multiplier=-1)

                    def more_constants():
                        pool.memset(ones_bf[:], 1.0)
                        pool.iota(expert_no[:], [[1, E]], 0, 0, allow_small_or_imprecise_dtypes=True)
                        pool.iota(id_f[:], [[P, T]], 0, 1, allow_small_or_imprecise_dtypes=True)
                        pool.iota(carry[:], [[1, E]], 0, 0, allow_small_or_imprecise_dtypes=True)
                        pool.iota(block_no[:], [[1, NBLOCKS]], 0, 0, allow_small_or_imprecise_dtypes=True)
                        pool.iota(odd_blocks[:].rearrange("p (h q) -> p h q", q=2), [[16 * T, (NBLOCKS + 1) // 2], [16 * T, 2]],
                                  -16 * T, 0, allow_small_or_imprecise_dtypes=True)
                        pool.iota(pad_id[:], [[1, T]], TOKENS, T, allow_small_or_imprecise_dtypes=True).then_inc(pool_step, 1)
                        pool.wait_ge(pool_step, 4)
                        pool.tensor_scalar(carry[:], carry[:], float(REGION), float(BLOCK), ALU.mult, ALU.add).then_inc(consts_made, 1)
                        pool.wait_ge(rows_zeroed, 1)
                        pool.tensor_copy(pad[:, :, ID].bitcast(U32), pad_id[:]).then_inc(pad_made, 1)

                    def store_padding():
                        pool.wait_ge(pad_made, 1)
                        pool.dma_start(tiles(out, G), pad[:, :, 0:D]).then_inc(scattered[1], 16)
                        for at in [e * REGION for e in range(E)] + [DUMMY]:
                            pool.dma_start(rows_dram[at:at + BLOCK, :].rearrange("(p t) r -> p (t r)", t=T),
                                           pad.rearrange("p t r -> p (t r)")).then_inc(scattered[1], 16)

                    def neg_of_mask(g):
                        wait_apart(pool, adj_loaded, 16 * g + 16)
                        pool.tensor_scalar(neg_mask[:], adj_t[:], -NEG, NEG, ALU.mult, ALU.add).then_inc(negmask_ready, 1)

                    def root(n, g, read):
                        wait_apart(pool, var_ready[n], g + 1)
                        if not (isinstance(g, int) and g == 0):
                            pool.wait_ge(read, g)
                        pool.tensor_tensor(rstd[n][:], var_eps[n][:], minus_half[:], ALU.pow).then_inc(root_step[n], 1)
                        pool.wait_ge(root_step[n], g + 1)
                        pool.tensor_tensor(norm_bias[n][:], neg_mean[n][:], rstd[n][:], ALU.mult).then_inc(rstd_ready[n], 1)

                    def write_ids(g, q, pair):
                        if not early(g, 1):
                            wait_apart(pool, scattered[q], rows_of(q, pair))
                        pool.tensor_copy(rows[:, q, :, ID].bitcast(U32), id_f[:]).then_inc(id_ready, 1)
                        wait_apart(pool, id_ready, g + 1)
                        pool.tensor_scalar(id_f[:], id_f[:], 1.0, float(N), ALU.mult, ALU.add).then_inc(id_step, 1)

                    def base(g, q):
                        pool.wait_ge(x1_ready, 2 * g + 2)
                        pool.wait_ge(xn2_ready, g + 1)
                        pool.tensor_tensor(x1[:], x1[:], rows[:, q, :, 0:D], ALU.add).then_inc(base_ready, 1)

                    def scatter(g, q, some=range(T)):
                        wait_apart(pool, id_ready, g + 1)
                        wait_apart(pool, gates_ready, g + 1)
                        wait_apart(pool, slots_ready, g + 1)
                        for t in some:
                            for k in range(2):
                                pool.indirect_dma_start(
                                    rows_dram, bass.IndirectOffsetOnAxis(ap=slot[:, q, k, t:t + 1], axis=0),
                                    rows[:, q, t, :], None).then_inc(scattered[q], 16)

                    root("1", 0, xn_ready)
                    neg_of_mask(0)
                    more_constants()
                    root("1", 1, xn_ready)
                    store_padding()

                    def graph(g, q, pair, first=False, last=False, load_after=True):
                        if not early(g):
                            scatter(g - 2, 1 - q, range(T - 1))
                        if not first:
                            root("2", g - 1, xn2_ready)
                        if not early(g):
                            scatter(g - 2, 1 - q, range(T - 1, T))
                        if not first:
                            write_ids(g - 1, q, pair)
                            base(g - 1, q)
                        if load_after:
                            root("1", g + 2, xn_ready)
                        if not last:
                            wait_apart(pool, shift_ready, 4 * g + 4)
                            neg_of_mask(g + 1)

                    graph(0, 1, 0, first=True)
                    graph(1, 0, 0)
                    with pool.Fori(1, G // 2 - 1) as i:
                        graph(2 * i, 1, i - 1)
                        graph(2 * i + 1, 0, i)
                    graph(G - 2, 1, G // 2 - 2, load_after=False)
                    graph(G - 1, 0, G // 2 - 1, last=True, load_after=False)
                    root("2", G - 1, xn2_ready)
                    write_ids(G - 1, 1, G // 2 - 1)
                    scatter(G - 2, 0)
                    base(G - 1, 1)
                    scatter(G - 1, 1)
                    for q in range(2):
                        pool.wait_ge(scattered[q], rows_of(q, G // 2))

                @block.scalar
                def _(act):
                    act.dma_start(router_rows[:], router_w).then_inc(loaded, 16)
                    act.dma_start(b_rows[0:E, :], b1).then_inc(loaded, 16)
                    act.wait_ge(bias_zeroed, 1)
                    for row in (0, 32):
                        act.dma_start(bv_stage[row:row + 1, :], bv.rearrange("(o n) -> o n", o=1)).then_inc(loaded, 16)
                    for i, b in enumerate((bq, bk)):
                        act.dma_start(b_rows[E + i:E + i + 1, :], b.rearrange("(o n) -> o n", o=1)).then_inc(loaded, 16)
                    act.dma_start(bo_rows[:], bo.partition_broadcast(P)).then_inc(loaded, 16)

                    def weights_hi(some):
                        for n in some:
                            act.wait_ge(w_loaded[n], 16)
                            act.copy(w_hi[n][:].rearrange("p c n -> p (c n)"), w_stage[n]).then_inc(hi_made, 1)

                    def norm(n, dst, src):
                        for t in range(T):
                            i = act.activation(dst[:, t, 0:D], src[:, t, :], ACT.Identity, bias=norm_bias[n][:, t:t + 1],
                                               scale=rstd[n][:, t:t + 1])
                        return i

                    def apply1(g, first=False):
                        act.wait_ge(rstd_ready["1"], g + 1)
                        if not first:
                            act.wait_ge(xnT_psum, 2 * g)
                        norm("1", xn, x_norm).then_inc(xn_ready, 1)

                    def apply2(g, q, pair):
                        act.wait_ge(rstd_ready["2"], g + 1)
                        if not early(g, 1):
                            act.wait_ge(scattered[q], rows_of(q, pair))
                        norm("2", rows[:, q], x1).then_inc(xn2_ready, 1)

                    def xnT(g, c):
                        act.wait_ge(xnT_psum, 2 * g + c + 1)
                        act.copy(xnT_hi[:, c, :], bank[2 + c][:]).then_inc(xnT_hi_ready, 1)

                    def qk(g, u):
                        act.wait_ge(qk_psum, 4 * g + u + 1)
                        if not early(g, 1):
                            act.wait_ge(probT_psum, 4 * g)
                        act.activation(qk_f[:, u, :], bank[4 + u][:], ACT.Relu,
                                       bias=bias_qk[:, u // C, u % C:u % C + 1]).then_inc(qk_ready, 1)

                    apply1(0, True)
                    weights_hi("qkv")
                    act.wait_ge(loaded, 16 * SMALL_LOADS)
                    act.copy(bias_v[:], bv_stage).then_inc(hi_made, 1)
                    for c in range(C):
                        xnT(0, c)
                    weights_hi("o")
                    act.wait_ge(lo_made, 5)
                    act.wait_ge(router_made, 1)
                    for u in range(2 * C):
                        qk(0, u)

                    def graph(g, q, pair, first=False, last=False):
                        if not last:
                            apply1(g + 1)
                        if not early(g):
                            route_exp(g - 2)
                        if not first:
                            act.wait_ge(inv_ready, g)
                        def v_of(i):
                            act.wait_ge(v_psum, 2 * g + i + 1)
                            act.activation(v_hi[:, 2 * i:2 * i + 2, :].rearrange("p t d -> p (t d)"), bank[i][:],
                                           ACT.Relu).then_inc(v_hi_ready, 1)

                        for t in range(T):
                            act.wait_ge(shift_ready, 4 * g + t + 1)
                            act.activation(prob[:, t, :], prob[:, t, :], ACT.Exp, bias=neg_max[:, t:t + 1], scale=-1.0,
                                           accum_out=row_sum[:, t:t + 1]).then_inc(prob_ready, 1)
                        for i in range(2):
                            v_of(i)
                        for m in range(T):
                            act.wait_ge(probT_psum, 4 * g + m + 1)
                            act.copy(probT_hi[:, m, :], bank[4 + m][:]).then_inc(probT_hi_ready, 1)
                            if 1 <= m <= C and not last:
                                xnT(g + 1, m - 1)
                        for c in range(C):
                            act.wait_ge(o_psum, 2 * g + c + 1)
                            act.copy(oT_hi[:, c, :], bank[c][:]).then_inc(o_hi_ready, 1)
                        if not first:
                            apply2(g - 1, q, pair)
                        if not last:
                            qk(g + 1, 0)
                            qk(g + 1, 1)
                        if not first:
                            route_in(g - 1)
                        if not last:
                            qk(g + 1, 2)
                        if not last:
                            qk(g + 1, 3)
                        if not first:
                            route_logits(g - 1)

                    def route_in(g):
                        for c in range(C):
                            act.wait_ge(xn2T_psum, 2 * g + c + 1)
                            act.copy(xn2T[:, c, :], bank[2 + c][:]).then_inc(xn2T_ready, 1)

                    def route_logits(g):
                        act.wait_ge(logitsT_psum, g + 1)
                        act.copy(logitsT[:], bank[2][0:E, :]).then_inc(logitsT_ready, 1)

                    def route_exp(g):
                        act.wait_ge(expo_in, g + 1)
                        act.activation(expo[:], shifted[:], ACT.Exp).then_inc(expo_ready, 1)

                    graph(0, 1, 0, first=True)
                    graph(1, 0, 0)
                    with act.Fori(1, G // 2 - 1) as i:
                        graph(2 * i, 1, i - 1)
                        graph(2 * i + 1, 0, i)
                    graph(G - 2, 1, G // 2 - 2)
                    graph(G - 1, 0, G // 2 - 1, last=True)
                    def experts(some):
                        act.wait_ge(experts_loaded, 16 * (2 * E + 1))
                        act.wait_ge(o_psum, 2 * G)
                        for n in some:
                            act.copy(w12_hi[:, n // 2, n % 2, :], w12_lo[:, n // 2, n % 2, :].bitcast(F32)).then_inc(experts_hi, 1)

                    experts(range(0, 4))
                    apply2(G - 1, 1, G // 2 - 1)
                    route_exp(G - 2)
                    experts(range(4, 6))
                    route_in(G - 1)
                    experts(range(6, 12))
                    route_logits(G - 1)
                    route_exp(G - 1)
                    experts(range(12, 2 * E))

                @block.vector
                def _(dve):
                    dve.memset(bv_stage, 0.0).then_inc(bias_zeroed, 1)
                    dve.memset(ones[:].bitcast(F32), 1.0)
                    dve.memset(rows[:], 0.0).then_inc(rows_zeroed, 1)

                    def weights_lo(some, done):
                        for i, n in enumerate(some):
                            dve.wait_ge(hi_made, done + i + 1)
                            dve.tensor_tensor(w_lo[n][:].rearrange("p c n -> p (c n)"), w_stage[n],
                                              w_hi[n][:].bitcast(F32).rearrange("p c n -> p (c n)"), ALU.subtract).then_inc(lo_made, 1)

                    def lo_of(dst, src, hi, relu):
                        if relu:
                            return dve.scalar_tensor_tensor(dst, src, 0.0, hi.bitcast(F32), ALU.max, ALU.subtract)
                        return dve.tensor_tensor(dst, src, hi.bitcast(F32), ALU.subtract)

                    def norm_stats(n, src, g, first=False):
                        for t in range(T):
                            i = dve.bn_stats(st[n][:, t, :], src[:, t, :])
                        i.then_inc(stats_step[n], 1)
                        wait_apart(dve, stats_step[n], 2 * g + 1)
                        for t in range(T):
                            i = dve.bn_aggr(mv[n][:, t, :], st[n][:, t, :])
                        i.then_inc(stats_step[n], 1)
                        if not first:
                            dve.wait_ge(rstd_ready[n], g)
                        dve.wait_ge(stats_step[n], 2 * g + 2)
                        dve.tensor_scalar(neg_mean[n][:], mv[n][:, :, 0], -1.0, None, ALU.mult)
                        dve.tensor_scalar(var_eps[n][:], mv[n][:, :, 1], EPS, None, ALU.add).then_inc(var_ready[n], 1)

                    def stats1(g, first=False):
                        dve.wait_ge(xnorm_loaded, 16 * g + 16)
                        norm_stats("1", x_norm, g, first)

                    def stats2(g):
                        dve.wait_ge(x1_ready, 2 * g + 2)
                        norm_stats("2", x1, g, early(g, 1))

                    def xnT(g, c):
                        dve.wait_ge(xnT_hi_ready, 2 * g + c + 1)
                        lo_of(xnT_lo[:, c, :], bank[2 + c][:], xnT_hi[:, c, :], False).then_inc(xnT_lo_ready, 1)

                    def qk(g, u):
                        dve.wait_ge(qk_ready, 4 * g + u + 1)
                        dve.tensor_copy(qk_hi[:, u, :], qk_f[:, u, :]).then_inc(qk_hi_ready, 1)
                        dve.wait_ge(qk_hi_ready, 4 * g + u + 1)
                        lo_of(qk_lo[:, u, :], qk_f[:, u, :], qk_hi[:, u, :], False).then_inc(qk_lo_ready, 1)

                    def wide(ap):
                        return ap.to_broadcast([P, T, E])

                    def route_choose(g):
                        step = [0]

                        def then(i):
                            step[0] += 1
                            i.then_inc(route_step, 1)
                            dve.wait_ge(route_step, ROUTE * g + step[0])

                        dve.wait_ge(logits_psum, g + 1)
                        step[0] += 1
                        dve.tensor_copy(logits[:].rearrange("p t e -> p (t e)"), bank[3][:, 0:T * E]).then_inc(route_step, 1)
                        wait_apart(dve, route_step, ROUTE * g + step[0])
                        for t in range(T):
                            i = dve.max(top8[:, t, :], logits[:, t, :])
                        then(i)
                        dve.tensor_tensor(shifted[:], logits[:], wide(top8[:, :, 0:1]), ALU.subtract).then_inc(expo_in, 1)
                        for t in range(T):
                            i = dve.max_index(top8_at[:, t, :], top8[:, t, :], logits[:, t, :])
                        then(i)
                        then(dve.tensor_copy(top2_at[:], top8_at[:, :, 0:2]))
                        for k in range(2):
                            i = dve.tensor_tensor(is_top[:, k], expert_no[:].unsqueeze(1).to_broadcast([P, T, E]),
                                                  wide(top2_at[:, :, k:k + 1]), ALU.is_equal)
                        then(i)
                        dve.tensor_tensor(chosen_bf[:], is_top[:, 0], is_top[:, 1], ALU.add).then_inc(chosen_ready, 1)
                        assert step[0] == CHOOSE

                    def gate_sums(g):
                        dve.wait_ge(expo_ready, g + 1)
                        dve.wait_ge(chosen_ready, g + 1)
                        dve.tensor_reduce(gate_sum[:, 0, :], expo[:], AX.X, ALU.add)
                        dve.tensor_tensor(gates[:], expo[:], chosen_bf[:], ALU.mult).then_inc(route_step, 1)

                    def chosen_sum(g):
                        dve.wait_ge(route_step, ROUTE * g + CHOOSE + 1)
                        dve.tensor_reduce(gate_sum[:, 1, :], gates[:], AX.X, ALU.add).then_inc(route_step, 1)

                    def guard_sum(g):
                        dve.wait_ge(route_step, ROUTE * g + CHOOSE + 2)
                        dve.scalar_tensor_tensor(gate_sum[:, 2, :], gate_sum[:, 0, :], 1e-12, gate_sum[:, 1, :],
                                                 ALU.mult, ALU.max).then_inc(route_step, 1)

                    def invert_sum(g):
                        dve.wait_ge(route_step, ROUTE * g + CHOOSE + 3)
                        dve.reciprocal(gate_sum[:, 3, :], gate_sum[:, 2, :]).then_inc(route_step, 1)

                    def weights_and_ranks(g, q):
                        dve.wait_ge(route_step, ROUTE * g + CHOOSE + 4)
                        dve.tensor_tensor(rows[:, q, :, GATE:GATE + E], gates[:], wide(gate_sum[:, 3, :].unsqueeze(2)),
                                          ALU.mult).then_inc(gates_ready, 1)
                        dve.wait_ge(rank_psum, g + 1)
                        ranks = bank[2][:, 0:T * E].rearrange("p (t e) -> p t e", t=T)
                        dve.tensor_tensor(place[:], ranks, carry[:].unsqueeze(1).to_broadcast([P, T, E]),
                                          ALU.add).then_inc(route_step, 1)

                    def places(g):
                        dve.wait_ge(route_step, ROUTE * g + CHOOSE + 5)
                        dve.tensor_tensor(carry[:], carry[:], bank[2][:, T * E:(T + 1) * E], ALU.add).then_inc(ranks_read, 1)
                        for k in range(2):
                            i = dve.tensor_tensor(place_top[:, k], place[:], is_top[:, k], ALU.mult)
                        i.then_inc(route_step, 1)

                    def places_top(g):
                        dve.wait_ge(route_step, ROUTE * g + CHOOSE + 6)
                        dve.tensor_reduce(slot_f[:], place_top[:], AX.X, ALU.add).then_inc(route_step, 1)

                    def slots_out(g, q):
                        dve.wait_ge(route_step, ROUTE * g + ROUTE)
                        dve.tensor_copy(slot[:, q], slot_f[:]).then_inc(slots_ready, 1)

                    def finish_routing(g, q):
                        gate_sums(g)
                        chosen_sum(g)
                        guard_sum(g)
                        invert_sum(g)
                        weights_and_ranks(g, q)
                        places(g)
                        places_top(g)
                        slots_out(g, q)

                    stats1(0, True)
                    weights_lo("qkv", 0)
                    dve.wait_ge(hi_made, 4)
                    dve.tensor_tensor(bias_v[32:33, :], bv_stage[32:33, :], bias_v[32:33, :].bitcast(F32),
                                      ALU.subtract).then_inc(lo_made, 1)
                    for c in range(C):
                        xnT(0, c)
                    weights_lo("o", 4)
                    dve.wait_ge(router_psum, 1)
                    dve.tensor_copy(router_t[:].rearrange("p c e -> p (c e)"), bank[7][:, 0:C * E])
                    biases = bank[7][:, C * E:C * E + C * (E + 2)].rearrange("p (c e) -> p e c", c=C)
                    dve.tensor_copy(b1_all[:], biases[:, 0:E, :])
                    dve.tensor_copy(bias_qk[:], biases[:, E:E + 2, :]).then_inc(router_made, 1)
                    for u in range(2 * C):
                        qk(0, u)
                    stats1(1)
                    dve.wait_ge(consts_made, 1)

                    def graph(g, q, first=False, last=False, load_after=True):
                        if not first:
                            dve.wait_ge(probT_psum, 4 * g)
                        dve.wait_ge(adj_loaded, 16 * g + 16)

                        def times_mask(t):
                            dve.wait_ge(score_psum, 4 * g + t + 1)
                            dve.scalar_tensor_tensor(
                                prob[:, t, :], bank[4 + t][:], -1.0, adj_t[:, t, :], ALU.mult, ALU.mult).then_inc(masked, 1)

                        def add_mask(t):
                            wait_apart(dve, masked, 4 * g + t + 1)
                            dve.tensor_tensor_reduce(prob[:, t, :], prob[:, t, :], neg_mask[:, t, :], 1.0, BIG, ALU.add,
                                                     ALU.min, neg_max[:, t:t + 1]).then_inc(shift_ready, 1)

                        late = not early(g)
                        times_mask(0)
                        dve.wait_ge(negmask_ready, g + 1)
                        if late:
                            gate_sums(g - 2)
                        times_mask(1)
                        if late:
                            chosen_sum(g - 2)
                        add_mask(0)
                        if late:
                            guard_sum(g - 2)
                        times_mask(2)
                        if late:
                            invert_sum(g - 2)
                        add_mask(1)
                        times_mask(3)
                        add_mask(2)
                        add_mask(3)
                        if late:
                            weights_and_ranks(g - 2, 1 - q)
                        if not first:
                            residual(g - 1, 0)
                        if late:
                            places(g - 2)
                        if not first:
                            residual(g - 1, 1)
                        rest_of_v(g, 0)
                        if late:
                            places_top(g - 2)
                        rest_of_v(g, 1)
                        if late:
                            slots_out(g - 2, 1 - q)
                        for m in range(T):
                            dve.wait_ge(probT_hi_ready, 4 * g + m + 1)
                            lo_of(probT_lo[:, m, :], bank[4 + m][:], probT_hi[:, m, :], False).then_inc(probT_lo_ready, 1)
                            if 1 <= m <= C and not last:
                                xnT(g + 1, m - 1)
                        dve.reciprocal(row_inv[:], row_sum[:]).then_inc(inv_ready, 1)
                        if not first:
                            stats2(g - 1)
                        if load_after:
                            stats1(g + 2)
                        for c in range(C):
                            dve.wait_ge(o_hi_ready, 2 * g + c + 1)
                            lo_of(oT_lo[:, c, :], bank[c][:], oT_hi[:, c, :], False).then_inc(o_lo_ready, 1)
                        if not last:
                            for u in range(2 * C):
                                qk(g + 1, u)
                        projected(g, 0)
                        if not first and not last:
                            route_choose(g - 1)
                        projected(g, 1)

                    def rest_of_v(g, i):
                        dve.wait_ge(v_hi_ready, 2 * g + i + 1)
                        lo_of(v_lo[:, 2 * i:2 * i + 2, :].rearrange("p t d -> p (t d)"), bank[i][:],
                              v_hi[:, 2 * i:2 * i + 2, :].rearrange("p t d -> p (t d)"), True).then_inc(v_lo_ready, 1)

                    def projected(g, i):
                        dve.wait_ge(inv_ready, g + 1)
                        dve.wait_ge(y_psum, 2 * g + i + 1)
                        for j in range(2):
                            t = 2 * i + j
                            dve.scalar_tensor_tensor(y_sb[:, t, :], bank[i][:, j * D:(j + 1) * D], row_inv[:, t:t + 1],
                                                     bo_rows[:], ALU.mult, ALU.add).then_inc(y_ready, 1)

                    def residual(g, i):
                        if not early(g, 1):
                            dve.wait_ge(base_stored, 16 * g)
                        dve.wait_ge(xres_loaded, 16 * g + 16)
                        dve.wait_ge(y_ready, 4 * g + 2 * i + 2)
                        dve.scalar_tensor_tensor(x1[:, 2 * i:2 * i + 2, :], y_sb[:, 2 * i:2 * i + 2, :], 0.0,
                                                 x_res[:, 2 * i:2 * i + 2, :], ALU.max, ALU.add).then_inc(x1_ready, 1)

                    graph(0, 1, first=True)
                    graph(1, 0)
                    with dve.Fori(1, G // 2 - 1) as i:
                        graph(2 * i, 1)
                        graph(2 * i + 1, 0)
                    graph(G - 2, 1, load_after=False)
                    graph(G - 1, 0, last=True, load_after=False)
                    for i in range(2):
                        residual(G - 1, i)
                    stats2(G - 1)
                    route_choose(G - 2)

                    def experts(some):
                        for n in some:
                            dve.wait_ge(experts_hi, n + 1)
                            dve.tensor_tensor(w12_lo[:, n // 2, n % 2, :], w12_lo[:, n // 2, n % 2, :].bitcast(F32),
                                              w12_hi[:, n // 2, n % 2, :].bitcast(F32), ALU.subtract)

                    finish_routing(G - 2, 0)
                    experts(range(0, 9))
                    route_choose(G - 1)
                    finish_routing(G - 1, 1)

                    step = [0]

                    def then(i):
                        step[0] += 1
                        i.then_inc(table_step, 1)
                        dve.wait_ge(table_step, step[0])

                    def over_blocks(ap):
                        return ap.unsqueeze(1).to_broadcast([P, NBLOCKS, E])

                    def over_experts(ap):
                        return ap.unsqueeze(2).to_broadcast([P, NBLOCKS, E])

                    FIRST, COUNT, BLOCKS, END, START = range(5)
                    dve.wait_ge(ranks_read, G)
                    then(dve.tensor_scalar(table[:, FIRST, :], expert_no[:], float(REGION), float(BLOCK), ALU.mult, ALU.add))
                    then(dve.tensor_tensor(table[:, COUNT, :], carry[:], table[:, FIRST, :], ALU.subtract))
                    then(dve.tensor_scalar(table_i[:, 0, :], table[:, COUNT, :], float(BLOCK - 1), None, ALU.add))
                    then(dve.tensor_scalar(table_i[:, 2, :], table_i[:, 0, :], 9, None, ALU.logical_shift_right))
                    then(dve.tensor_copy(table[:, BLOCKS, :], table_i[:, 2, :]))
                    then(dve.tensor_copy(table[:, END, :], table[:, BLOCKS, :]))
                    for e in range(1, E):
                        then(dve.tensor_tensor(table[:, END, e:e + 1], table[:, END, e - 1:e], table[:, BLOCKS, e:e + 1], ALU.add))
                    then(dve.tensor_tensor(table[:, START, :], table[:, END, :], table[:, BLOCKS, :], ALU.subtract))
                    then(dve.scalar_tensor_tensor(table[:, START, :], table[:, START, :], float(BLOCK), carry[:],
                                                  ALU.mult, ALU.add))
                    then(dve.tensor_tensor(ended, over_experts(block_no[:]), over_blocks(table[:, END, :]), ALU.is_ge))
                    dve.tensor_scalar(inside[:, :, 0:1], ended[:, :, 0:1], -1.0, 1.0, ALU.mult, ALU.add)
                    then(dve.tensor_tensor(inside[:, :, 1:E], ended[:, :, 0:E - 1], ended[:, :, 1:E], ALU.subtract))
                    then(dve.tensor_scalar(block_at[:], block_no[:], -float(BLOCK), float(-DUMMY - BLOCK), ALU.mult, ALU.add))
                    then(dve.tensor_tensor(start_of, over_experts(block_at[:]), over_blocks(table[:, START, :]), ALU.add))
                    then(dve.tensor_tensor(start_of, start_of, inside, ALU.mult))
                    then(dve.tensor_reduce(block_e[:, 0, :], start_of, AX.X, ALU.add))
                    then(dve.tensor_scalar(first_row[:], block_e[:, 0, :], float(DUMMY), None, ALU.add))
                    then(dve.tensor_reduce(block_e[:, 1, :], ended, AX.X, ALU.add))
                    then(dve.tensor_scalar(expert_of[:], block_e[:, 1, :], float(E - 1), None, ALU.min))
                    later = slice(1, NBLOCKS)
                    then(dve.tensor_tensor(block_e[:, 2, later], block_e[:, 1, later], block_e[:, 1, 0:NBLOCKS - 1], ALU.not_equal))
                    then(dve.scalar_tensor_tensor(block_e[:, 2, later], block_e[:, 1, later], float(E), block_e[:, 2, later],
                                                  ALU.is_equal, ALU.max))
                    then(dve.scalar_tensor_tensor(added_before[:, later], block_e[:, 2, later], float(16 * T),
                                                  odd_blocks[:, later], ALU.mult, ALU.add))
                    experts(range(9, 2 * E))

                @block.tensor
                def _(pe):
                    pe.wait_ge(ident_made, 1)

                    def split3(dst, a_hi, a_lo, b_hi, b_lo, start, stop):
                        pe.matmul(dst, a_hi, b_hi, start=start, stop=False)
                        pe.matmul(dst, a_hi, b_lo, start=False, stop=False)
                        return pe.matmul(dst, a_lo, b_hi, start=False, stop=stop)

                    def xnT(g):
                        pe.wait_ge(xn_ready, g + 1)
                        for c in range(C):
                            for t in range(T):
                                i = pe.transpose(bank[2 + c][:, t * P:(t + 1) * P], xn[:, t, c * P:(c + 1) * P], ident[:])
                            i.then_inc(xnT_psum, 1)

                    def qk(g, u):
                        n, h = "qk"[u // C], u % C
                        dst = bank[4 + u][:]
                        for c in range(C):
                            i = split3(dst, w_hi[n][:, c, h * P:(h + 1) * P], w_lo[n][:, c, h * P:(h + 1) * P],
                                       xnT_hi[:, c, :], xnT_lo[:, c, :], c == 0, c == C - 1)
                        i.then_inc(qk_psum, 1)

                    def route_in(g, q):
                        pe.wait_ge(xn2_ready, g + 1)
                        for c in range(C):
                            for t in range(T):
                                i = pe.transpose(bank[2 + c][:, t * P:(t + 1) * P], rows[:, q, t, c * P:(c + 1) * P], ident[:])
                            i.then_inc(xn2T_psum, 1)

                    def route_logitsT(g):
                        pe.wait_ge(xn2T_ready, 2 * g + 2)
                        for c in range(C):
                            i = pe.matmul(bank[2][0:E, :], router_t[:, c, :], xn2T[:, c, :], start=(c == 0), stop=(c == C - 1))
                        i.then_inc(logitsT_psum, 1)

                    def route_logits(g):
                        wait_apart(pe, logitsT_ready, g + 1)
                        for t in range(T):
                            i = pe.transpose(bank[3][:, t * E:(t + 1) * E], logitsT[:, t * P:(t + 1) * P], ident[0:E, 0:E])
                        i.then_inc(logits_psum, 1)

                    def route_ranks(g):
                        pe.wait_ge(chosen_ready, g + 1)
                        for t in range(T + 1):
                            dst = bank[2][:, t * E:(t + 1) * E]
                            if t < T:
                                i = pe.matmul(dst, before[:], chosen_bf[:, t, :], start=True, stop=(t == 0))
                            for s in range(t):
                                i = pe.matmul(dst, ones_bf[:], chosen_bf[:, s, :], start=(t == T and s == 0), stop=(s == t - 1))
                        i.then_inc(rank_psum, 1)

                    xnT(0)
                    pe.wait_ge(loaded, 16 * SMALL_LOADS)
                    for c in range(C):
                        pe.transpose(bank[7][:, c * E:(c + 1) * E], router_rows[:, c * P:(c + 1) * P], ident[0:E, 0:E])
                    for c in range(C):
                        at = C * E + c * (E + 2)
                        i = pe.transpose(bank[7][:, at:at + E + 2], b_rows[:, c * P:(c + 1) * P], ident[0:E + 2, 0:E + 2])
                    i.then_inc(router_psum, 1)
                    pe.wait_ge(lo_made, 4)
                    pe.wait_ge(router_made, 1)
                    pe.wait_ge(xnT_hi_ready, 2)
                    pe.wait_ge(xnT_lo_ready, 2)
                    for u in range(2 * C):
                        qk(0, u)

                    def graph(g, q, first=False, last=False):
                        pe.wait_ge(qk_hi_ready, 4 * g + 4)
                        pe.wait_ge(qk_lo_ready, 4 * g + 4)
                        for t in range(T):
                            if t == 2 and not early(g):
                                route_ranks(g - 2)
                            for c in range(C):
                                i = split3(bank[4 + t][:], qk_hi[:, c, t * P:(t + 1) * P], qk_lo[:, c, t * P:(t + 1) * P],
                                           qk_hi[:, C + c, :], qk_lo[:, C + c, :], c == 0, c == C - 1)
                            i.then_inc(score_psum, 1)
                        for i2 in range(2):
                            if not first:
                                pe.wait_ge(y_ready, 4 * g - 2 + 2 * i2)
                            for j in range(2):
                                t = 2 * i2 + j
                                dst = bank[i2][:, j * D:(j + 1) * D]
                                pe.matmul(dst, ones[:], bias_v[:], start=True, stop=False)
                                for c in range(C):
                                    i = split3(dst, xnT_hi[:, c, t * P:(t + 1) * P], xnT_lo[:, c, t * P:(t + 1) * P],
                                               w_hi["v"][:, c, :], w_lo["v"][:, c, :], False, c == C - 1)
                            i.then_inc(v_psum, 1)
                        pe.wait_ge(prob_ready, 4 * g + 4)
                        for m in range(T):
                            for t in range(T):
                                i = pe.transpose(bank[4 + m][:, t * P:(t + 1) * P], prob[:, t, m * P:(m + 1) * P], ident[:])
                            i.then_inc(probT_psum, 1)
                        if not last:
                            if not early(g):
                                pe.wait_ge(ranks_read, g - 1)
                            xnT(g + 1)
                        pe.wait_ge(v_lo_ready, 2 * g + 2)
                        for m in range(T):
                            pe.wait_ge(probT_hi_ready, 4 * g + m + 1)
                            pe.wait_ge(probT_lo_ready, 4 * g + m + 1)
                            for c in range(C):
                                i = split3(bank[c][:], v_hi[:, m, c * P:(c + 1) * P], v_lo[:, m, c * P:(c + 1) * P],
                                           probT_hi[:, m, :], probT_lo[:, m, :], m == 0, m == T - 1)
                                if m == T - 1:
                                    i.then_inc(o_psum, 1)
                        if last:
                            for i2 in range(2):
                                project(g, i2)
                            route_in(g - 1, q)
                            route_logitsT(g - 1)
                            route_logits(g - 1)
                            return
                        pe.wait_ge(xnT_hi_ready, 2 * g + 4)
                        pe.wait_ge(xnT_lo_ready, 2 * g + 4)
                        for u in range(3):
                            qk(g + 1, u)
                        if not first:
                            route_in(g - 1, q)
                        qk(g + 1, 3)
                        if not first:
                            route_logitsT(g - 1)
                        project(g, 0)
                        if not first:
                            route_logits(g - 1)
                        project(g, 1)

                    def project(g, i2):
                        if early(g, 1):
                            pe.wait_ge(lo_made, 5)
                        pe.wait_ge(o_hi_ready, 2 * g + 2)
                        pe.wait_ge(o_lo_ready, 2 * g + 2)
                        for j in range(2):
                            t = 2 * i2 + j
                            dst = bank[i2][:, j * D:(j + 1) * D]
                            for c in range(C):
                                i = split3(dst, oT_hi[:, c, t * P:(t + 1) * P], oT_lo[:, c, t * P:(t + 1) * P],
                                           w_hi["o"][:, c, :], w_lo["o"][:, c, :], c == 0, c == C - 1)
                        i.then_inc(y_psum, 1)

                    graph(0, 1, first=True)
                    graph(1, 0)
                    with pe.Fori(1, G // 2 - 1) as i:
                        graph(2 * i, 1)
                        graph(2 * i + 1, 0)
                    graph(G - 2, 1)
                    graph(G - 1, 0, last=True)
                    route_ranks(G - 2)
                    pe.wait_ge(ranks_read, G - 1)
                    route_in(G - 1, 1)
                    route_logitsT(G - 1)
                    route_logits(G - 1)
                    route_ranks(G - 1)

        with ExitStack() as ph:
            SLOTS = 4
            now1 = sb(ph, "now1", [P, 2, 2, MAT], F32R)
            b1_now = sb(ph, "b1_now", [P, 2, C], F32)
            xrow = sb(ph, "xrow", [P, SLOTS, T, ROW], F32)
            token = sb(ph, "token", [P, SLOTS, T], U32)
            gate = sb(ph, "gate", [P, SLOTS, T], F32)
            y = sb(ph, "y", [P, SLOTS, T, D], F32)
            xT_hi = sb(ph, "xT_hi", [P, C, BLOCK], F32R)
            xT_lo = sb(ph, "xT_lo", [P, C, BLOCK], F32R)
            h_sb = sb(ph, "h_sb", [P, 2, C, BLOCK], F32)
            h_hi = sb(ph, "h_hi", [P, 2, C, BLOCK], F32R)
            h_lo = sb(ph, "h_lo", [P, 2, C, BLOCK], F32R)

            xrow_loaded = [sem(f"xrow_loaded{s}") for s in range(SLOTS)]
            picked = sem("picked")
            now1_hi = sem("now1_hi")
            now1_lo = sem("now1_lo")
            xT_psum = sem("xT_psum")
            xT_hi_done = sem("xT_hi_done")
            xT_lo_done = sem("xT_lo_done")
            h_psum = sem("h_psum")
            h_ready = sem("h_ready")
            h_hi_done = sem("h_hi_done")
            h_lo_done = sem("h_lo_done")
            ye_psum = sem("ye_psum")
            ye_ready = sem("ye_ready")
            y_weighed = sem("y_weighed")
            added = [sem(f"added{q}") for q in range(2)]

            def expert(eng, j):
                return eng.value_load(expert_of[0:1, bass.ds(j, 1)], min_val=0, max_val=E - 1)

            LOOP = (NBLOCKS - 3) // SLOTS

            with nc.Block() as block:

                @block.sync
                def _(sp):
                    def load_rows(j, s):
                        at = sp.value_load(first_row[0:1, bass.ds(j, 1)], min_val=0, max_val=DUMMY)
                        if not early(j, SLOTS):
                            wait_apart(sp, xT_psum, 2 * (j - SLOTS) + 2)
                            wait_apart(sp, picked, j - SLOTS + 1)
                        sp.dma_start(xrow[:, s].rearrange("p t r -> p (t r)"),
                                     rows_dram[bass.ds(at, BLOCK), :].rearrange("(p t) r -> p (t r)", t=T)).then_inc(xrow_loaded[s], 16)

                    for j in range(SLOTS):
                        load_rows(j, j)
                    with sp.Fori(1, LOOP) as i:
                        for s in range(SLOTS):
                            load_rows(SLOTS * i + s, s)
                    for j in range(SLOTS * LOOP, NBLOCKS):
                        load_rows(j, j % SLOTS)

                @block.gpsimd
                def _(pool):
                    def add_rows(j, s, turn):
                        q = s % 2
                        before_it = 2 * turn + s // 2
                        if not early(j, 2):
                            wait_apart(pool, added[q], 16 * T * before_it)
                        if not early(j, SLOTS):
                            must = pool.value_load(added_before[0:1, bass.ds(j, 1)], min_val=16 * T, max_val=16 * T * NBLOCKS)
                            wait_apart(pool, added[1 - q], must)
                        elif not early(j, 1):
                            pool.wait_ge(added[1 - q], 16 * T * ((j + 1) // 2))
                        wait_apart(pool, picked, j + 1)
                        wait_apart(pool, y_weighed, 2 * j + 2)
                        for t in range(T):
                            pool.indirect_dma_start(out, bass.IndirectOffsetOnAxis(ap=token[:, s, t:t + 1], axis=0),
                                                    y[:, s, t, :], None, compute_op=ALU.add).then_inc(added[q], 16)

                    for j in range(SLOTS):
                        add_rows(j, j, 0)
                    with pool.Fori(1, LOOP) as i:
                        for s in range(SLOTS):
                            add_rows(SLOTS * i + s, s, i)
                    for j in range(SLOTS * LOOP, NBLOCKS):
                        add_rows(j, j % SLOTS, j // SLOTS)
                    pool.wait_ge(added[0], 16 * T * ((NBLOCKS + 1) // 2))
                    pool.wait_ge(added[1], 16 * T * (NBLOCKS // 2))

                @block.scalar
                def _(act):
                    def x_hi(j):
                        for c in range(C):
                            act.wait_ge(xT_psum, 2 * j + c + 1)
                            act.copy(xT_hi[:, c, :], bank[c][:]).then_inc(xT_hi_done, 1)

                    def w1_hi(j, q):
                        e = expert(act, j)
                        if not early(j, 2):
                            act.wait_ge(h_psum, 2 * (j - 2) + 2)
                        act.copy(now1[:, q, 0], w12_hi[:, bass.ds(e, 1), 0, :].bitcast(F32).rearrange("p o n -> p (o n)")).then_inc(now1_hi, 1)

                    def hidden(j, q):
                        act.wait_ge(now1_lo, j + 1)
                        if not early(j, 2):
                            act.wait_ge(h_lo_done, 2 * (j - 2) + 2)
                        for c in range(C):
                            act.wait_ge(h_psum, 2 * j + c + 1)
                            act.activation(h_sb[:, q, c, :], bank[2 + c][:], ACT.Gelu, bias=b1_now[:, q, c:c + 1]).then_inc(h_ready, 1)

                    def weigh(j, s):
                        act.wait_ge(picked, j + 1)
                        for i in range(2):
                            act.wait_ge(ye_ready, 2 * j + i + 1)
                            for t in (2 * i, 2 * i + 1):
                                k = act.activation(y[:, s, t, :], y[:, s, t, :], ACT.Copy, scale=gate[:, s, t:t + 1])
                            k.then_inc(y_weighed, 1)

                    def step(j, s, more=2):
                        if more >= 2:
                            w1_hi(j + 2, s % 2)
                        if more >= 1:
                            hidden(j + 1, 1 - s % 2)
                        if more >= 2:
                            x_hi(j + 2)
                        if not early(j, 1):
                            weigh(j - 1, (s - 1) % SLOTS)

                    w1_hi(0, 0)
                    w1_hi(1, 1)
                    x_hi(0)
                    hidden(0, 0)
                    x_hi(1)
                    for j in range(SLOTS + 1):
                        step(j, j % SLOTS)
                    with act.Fori(1, LOOP) as i:
                        for k in range(1, SLOTS + 1):
                            step(SLOTS * i + k, k % SLOTS)
                    for j in range(SLOTS * LOOP + 1, NBLOCKS):
                        step(j, j % SLOTS, min(2, NBLOCKS - 1 - j))
                    weigh(NBLOCKS - 1, (NBLOCKS - 1) % SLOTS)

                @block.vector
                def _(dve):
                    def w1_lo(j, q):
                        e = expert(dve, j)
                        if not early(j, 2):
                            dve.wait_ge(h_ready, 2 * (j - 2) + 2)
                        dve.tensor_copy(b1_now[:, q], b1_all[:, bass.ds(e, 1), :].rearrange("p o c -> p (o c)"))
                        dve.tensor_copy(now1[:, q, 1], w12_lo[:, bass.ds(e, 1), 0, :].bitcast(F32).rearrange("p o n -> p (o n)")).then_inc(now1_lo, 1)

                    def with_b2(j, s, turn):
                        e = expert(dve, j)
                        if not early(j, SLOTS):
                            dve.wait_ge(added[s % 2], 16 * T * (2 * turn + s // 2 - 1))
                        for i in range(2):
                            dve.wait_ge(ye_psum, 2 * j + i + 1)
                            dve.tensor_tensor(y[:, s, 2 * i:2 * i + 2, :], bank[4 + 2 * (s % 2) + i][:].rearrange("p (t d) -> p t d", t=2),
                                              b2_all[:, bass.ds(e, 1), :].to_broadcast([P, 2, D]), ALU.add).then_inc(ye_ready, 1)

                    def pick(j, s, turn):
                        e = expert(dve, j)
                        dve.wait_ge(xrow_loaded[s], 16 * turn + 16)
                        if not early(j, SLOTS):
                            dve.wait_ge(added[s % 2], 16 * T * (2 * turn + s // 2 - 1))
                        dve.tensor_copy(token[:, s], xrow[:, s, :, ID].bitcast(U32))
                        dve.tensor_copy(gate[:, s], xrow[:, s, :, bass.ds(e + GATE, 1)].rearrange("p t o -> p (t o)")).then_inc(picked, 1)

                    def x_lo(j):
                        for c in range(C):
                            dve.wait_ge(xT_hi_done, 2 * j + c + 1)
                            dve.tensor_tensor(xT_lo[:, c, :], bank[c][:], xT_hi[:, c, :].bitcast(F32),
                                              ALU.subtract).then_inc(xT_lo_done, 1)

                    def hidden_hi(j, q):
                        if not early(j, 2):
                            dve.wait_ge(ye_psum, 2 * (j - 2) + 2)
                        for c in range(C):
                            dve.wait_ge(h_ready, 2 * j + c + 1)
                            dve.tensor_copy(h_hi[:, q, c, :], h_sb[:, q, c, :]).then_inc(h_hi_done, 1)

                    def hidden_lo(j, q):
                        for c in range(C):
                            dve.wait_ge(h_hi_done, 2 * j + c + 1)
                            dve.tensor_tensor(h_lo[:, q, c, :], h_sb[:, q, c, :], h_hi[:, q, c, :].bitcast(F32),
                                              ALU.subtract).then_inc(h_lo_done, 1)

                    def step(j, s, turn, more=2):
                        q = s % 2
                        if not early(j, 1):
                            with_b2(j - 1, (s - 1) % SLOTS, turn - (1 if s == 0 else 0))
                        if more >= 2:
                            w1_lo(j + 2, q)
                        if more >= 1:
                            hidden_hi(j + 1, 1 - q)
                        if more >= 2:
                            x_lo(j + 2)
                        if more >= 1:
                            hidden_lo(j + 1, 1 - q)
                            pick(j + 1, (s + 1) % SLOTS, turn + (s + 1) // SLOTS)

                    w1_lo(0, 0)
                    w1_lo(1, 1)
                    x_lo(0)
                    hidden_hi(0, 0)
                    x_lo(1)
                    hidden_lo(0, 0)
                    pick(0, 0, 0)
                    for j in range(SLOTS + 1):
                        step(j, j % SLOTS, j // SLOTS)
                    with dve.Fori(1, LOOP) as i:
                        for k in range(1, SLOTS + 1):
                            step(SLOTS * i + k, k % SLOTS, i + k // SLOTS)
                    for j in range(SLOTS * LOOP + 1, NBLOCKS):
                        step(j, j % SLOTS, j // SLOTS, min(2, NBLOCKS - 1 - j))
                    with_b2(NBLOCKS - 1, (NBLOCKS - 1) % SLOTS, (NBLOCKS - 1) // SLOTS)

                @block.tensor
                def _(pe):
                    def split3(dst, a_hi, a_lo, b_hi, b_lo, start, stop):
                        pe.matmul(dst, a_hi, b_hi, start=start, stop=False)
                        pe.matmul(dst, a_hi, b_lo, start=False, stop=False)
                        return pe.matmul(dst, a_lo, b_hi, start=False, stop=stop)

                    def turn_rows(j, s, turn):
                        pe.wait_ge(xrow_loaded[s], 16 * turn + 16)
                        if not early(j, 1):
                            pe.wait_ge(xT_lo_done, 2 * j)
                        for c in range(C):
                            for t in range(T):
                                i = pe.transpose(bank[c][:, t * P:(t + 1) * P], xrow[:, s, t, c * P:(c + 1) * P], ident[:])
                            i.then_inc(xT_psum, 1)

                    def layer1(j, q):
                        pe.wait_ge(now1_hi, j + 1)
                        pe.wait_ge(now1_lo, j + 1)
                        pe.wait_ge(xT_hi_done, 2 * j + 2)
                        pe.wait_ge(xT_lo_done, 2 * j + 2)
                        if not early(j, 1):
                            pe.wait_ge(h_ready, 2 * j)
                        for h in range(C):
                            for c in range(C):
                                at = slice(c * D + h * P, c * D + (h + 1) * P)
                                i = split3(bank[2 + h][:], now1[:, q, 0, at], now1[:, q, 1, at],
                                           xT_hi[:, c, :], xT_lo[:, c, :], c == 0, c == C - 1)
                            i.then_inc(h_psum, 1)

                    def w2(half, e, at):
                        return half[:, bass.ds(e, 1), 1, at].rearrange("p o n -> p (o n)")

                    def layer2(j, q):
                        e = expert(pe, j)
                        pe.wait_ge(h_hi_done, 2 * j + 2)
                        pe.wait_ge(h_lo_done, 2 * j + 2)
                        if not early(j, 2):
                            pe.wait_ge(ye_ready, 2 * (j - 2) + 2)
                        for i2 in range(2):
                            for t in (2 * i2, 2 * i2 + 1):
                                dst = bank[4 + 2 * q + i2][:, (t % 2) * D:(t % 2 + 1) * D]
                                for c in range(C):
                                    at = slice(c * D, (c + 1) * D)
                                    i = split3(dst, h_hi[:, q, c, t * P:(t + 1) * P], h_lo[:, q, c, t * P:(t + 1) * P],
                                               w2(w12_hi, e, at), w2(w12_lo, e, at), c == 0, c == C - 1)
                            i.then_inc(ye_psum, 1)

                    def step(j, s, turn, more=2):
                        q = s % 2
                        if more >= 1:
                            layer1(j + 1, 1 - q)
                        if more >= 2:
                            turn_rows(j + 2, (s + 2) % SLOTS, turn + (s + 2) // SLOTS)
                        layer2(j, q)

                    turn_rows(0, 0, 0)
                    layer1(0, 0)
                    turn_rows(1, 1, 0)
                    for j in range(SLOTS + 1):
                        step(j, j % SLOTS, j // SLOTS)
                    with pe.Fori(1, LOOP) as i:
                        for k in range(1, SLOTS + 1):
                            step(SLOTS * i + k, k % SLOTS, i + k // SLOTS)
                    for j in range(SLOTS * LOOP + 1, NBLOCKS):
                        step(j, j % SLOTS, j // SLOTS, min(2, NBLOCKS - 1 - j))


_INS = ["x", "adj", "L0_gnn_Wv", "L0_gnn_bv", "L0_gnn_Wk", "L0_gnn_bk", "L0_gnn_Wq", "L0_gnn_bq", "L0_gnn_Wo",
        "L0_gnn_bo", "L0_ffn_router_w", "L0_ffn_w1", "L0_ffn_b1", "L0_ffn_w2", "L0_ffn_b2"]


def kernel(**inputs):
    import numpy as np
    import concourse.bacc as bacc
    from concourse.bass_utils import run_bass_kernel_spmd

    nc = bacc.Bacc("TRN2", target_bir_lowering=False, num_devices=1)
    arrays, args = {}, []
    for name in _INS:
        a = np.ascontiguousarray(inputs[name])
        arrays[f"in_{name}"] = a
        args.append(nc.dram_tensor(f"in_{name}", a.shape, mybir.dt.from_np(a.dtype), kind="ExternalInput").ap())
    g, n, d = inputs["x"].shape
    args.append(nc.dram_tensor("out_rows", [g * n + 512, d], F32, kind="ExternalOutput").ap())
    build_program(nc, *args)
    r = run_bass_kernel_spmd(nc, [arrays], core_ids=[0])
    return r.results[0]["out_rows"][:g * n].reshape(g, n, d)
```
